# Optimizing a Trainium2 kernel written in Bass

```python
import numpy as np
import jax
import jax.numpy as jnp

def _softmax(x, axis=-1):
    return jax.nn.softmax(x, axis=axis)

def _gelu(x):
    return jax.nn.gelu(x, approximate=True)

def _silu(x):
    return jax.nn.silu(x)

def _sigmoid(x):
    return jax.nn.sigmoid(x)

def _layernorm(x, axis=-1, eps=1e-05):
    m = jnp.mean(x, axis=axis, keepdims=True)
    v = jnp.var(x, axis=axis, keepdims=True)
    return (x - m) / jnp.sqrt(v + eps)

def _scatter_add(tgt, idx, src, axis=0):
    return tgt.at[idx].add(src)

def _segment_sum(src, seg, n):
    return jax.ops.segment_sum(src, seg, n)
kernel_name = 'mk_prb_d1_jaxref_r8_b47a8b'

def setup_inputs(seed: int=0):
    np.random.seed(seed)
    _w = jnp.asarray

    def _L0_attn_setup():
        import jax, jax.numpy as jnp
        import numpy as np
        B, T, D_MODEL = (4, 256, 256)
        NUM_HEADS, HEAD_SIZE = (16, 128)
        MODEL_SIZE = 256
        key = jax.random.key(seed)
        ks = jax.random.split(key, 9)
        s = 0.02 / np.sqrt(D_MODEL)
        so = 0.02 / np.sqrt(NUM_HEADS * HEAD_SIZE)
        return {'query': jax.random.normal(ks[0], (B, T, D_MODEL), jnp.float32), 'w_q': jax.random.normal(ks[1], (D_MODEL, NUM_HEADS * HEAD_SIZE), jnp.float32) * s, 'b_q': jnp.zeros((NUM_HEADS * HEAD_SIZE,), jnp.float32), 'w_k': jax.random.normal(ks[2], (D_MODEL, NUM_HEADS * HEAD_SIZE), jnp.float32) * s, 'b_k': jnp.zeros((NUM_HEADS * HEAD_SIZE,), jnp.float32), 'w_v': jax.random.normal(ks[3], (D_MODEL, NUM_HEADS * HEAD_SIZE), jnp.float32) * s, 'b_v': jnp.zeros((NUM_HEADS * HEAD_SIZE,), jnp.float32), 'w_o': jax.random.normal(ks[4], (NUM_HEADS * HEAD_SIZE, MODEL_SIZE), jnp.float32) * so, 'b_o': jnp.zeros((MODEL_SIZE,), jnp.float32)}
    _L0_attn_in = _L0_attn_setup()

    def _L0_ffn_setup():
        import jax, jax.numpy as jnp
        import numpy as np
        TOP_K = 4
        key = jax.random.key(seed)
        ks = jax.random.split(key, 8)
        B, S, H = (1, 128, 256)
        E, I = (60, 176)
        I_SH = 704
        s = 0.02
        return {'hidden_states': jax.random.normal(ks[0], (B, S, H), jnp.float32), 'gate_w': jax.random.normal(ks[1], (E, H), jnp.float32) * s, 'shared_gate_w': jax.random.normal(ks[2], (1, H), jnp.float32) * s, 'w13': jax.random.normal(ks[3], (E, 2 * I, H), jnp.float32) * s, 'w2': jax.random.normal(ks[4], (E, H, I), jnp.float32) * s, 'se_gate_up_w': jax.random.normal(ks[5], (2 * I_SH, H), jnp.float32) * s, 'se_down_w': jax.random.normal(ks[6], (H, I_SH), jnp.float32) * s}
    _L0_ffn_in = _L0_ffn_setup()
    _d = {'L0_attn_query': _L0_attn_in['query'], 'L0_attn_w_q': _L0_attn_in['w_q'], 'L0_attn_b_q': _L0_attn_in['b_q'], 'L0_attn_w_k': _L0_attn_in['w_k'], 'L0_attn_b_k': _L0_attn_in['b_k'], 'L0_attn_w_v': _L0_attn_in['w_v'], 'L0_attn_b_v': _L0_attn_in['b_v'], 'L0_attn_w_o': _L0_attn_in['w_o'], 'L0_attn_b_o': _L0_attn_in['b_o'], 'L0_ffn_gate_w': _L0_ffn_in['gate_w'], 'L0_ffn_shared_gate_w': _L0_ffn_in['shared_gate_w'], 'L0_ffn_w13': _L0_ffn_in['w13'], 'L0_ffn_w2': _L0_ffn_in['w2'], 'L0_ffn_se_gate_up_w': _L0_ffn_in['se_gate_up_w'], 'L0_ffn_se_down_w': _L0_ffn_in['se_down_w']}
    _x0 = _d['L0_attn_query']
    _d['L0_attn_query'] = jax.random.normal(jax.random.fold_in(jax.random.key(seed), 1), (2, 512, 256), dtype=_x0.dtype)
    del _x0
    return _d

def reference(L0_attn_query, L0_attn_w_q, L0_attn_b_q, L0_attn_w_k, L0_attn_b_k, L0_attn_w_v, L0_attn_b_v, L0_attn_w_o, L0_attn_b_o, L0_ffn_gate_w, L0_ffn_shared_gate_w, L0_ffn_w13, L0_ffn_w2, L0_ffn_se_gate_up_w, L0_ffn_se_down_w):

    def _L0_attn_ref(query, w_q, b_q, w_k, b_k, w_v, b_v, w_o, b_o):
        import jax, jax.numpy as jnp
        import numpy as np
        B, T, D_MODEL = (4, 256, 256)
        NUM_HEADS, HEAD_SIZE = (16, 128)
        MODEL_SIZE = 256
        B_, T_, _ = query.shape
        q = (query @ w_q + b_q).reshape(B_, T_, NUM_HEADS, HEAD_SIZE)
        k = (query @ w_k + b_k).reshape(B_, T_, NUM_HEADS, HEAD_SIZE)
        v = (query @ w_v + b_v).reshape(B_, T_, NUM_HEADS, HEAD_SIZE)
        logits = jnp.einsum('bthd,bThd->bhtT', q, k) * jax.lax.rsqrt(jnp.float32(HEAD_SIZE))
        i = jnp.arange(T_, dtype=jnp.int32)[:, None]
        j = jnp.arange(T_, dtype=jnp.int32)
        mask = (i >= j).astype(logits.dtype)
        logits = logits - 10000000000.0 * (1.0 - mask)
        weights = jax.nn.softmax(logits, axis=-1)
        attn = jnp.einsum('bhtT,bThd->bthd', weights, v).reshape(B_, T_, NUM_HEADS * HEAD_SIZE)
        out = attn @ w_o + b_o
        return out

    def _L0_ffn_ref(hidden_states, gate_w, shared_gate_w, w13, w2, se_gate_up_w, se_down_w):
        import jax, jax.numpy as jnp
        import numpy as np
        TOP_K = 4
        orig_shape = hidden_states.shape
        E, H = gate_w.shape
        I = w2.shape[2]
        x = hidden_states.reshape(-1, H)
        M = x.shape[0]
        gu = x @ se_gate_up_w.T
        I_sh = se_down_w.shape[1]
        shared = jax.nn.silu(gu[:, :I_sh]) * gu[:, I_sh:] @ se_down_w.T
        shared = shared * jax.nn.sigmoid(x @ shared_gate_w.T)
        logits = x @ gate_w.T
        probs = jax.nn.softmax(logits.astype(jnp.float32), axis=-1)
        weights, sel = jax.lax.top_k(probs, TOP_K)
        cw = jnp.zeros((M, E), jnp.float32).at[jnp.arange(M)[:, None], sel].add(weights)

        def step(acc, ews):
            w13_e, w2_e, cw_e = ews
            gu_e = x @ w13_e.T
            h = jax.nn.silu(gu_e[:, :I]) * gu_e[:, I:]
            return (acc + cw_e[:, None] * (h @ w2_e.T), None)
        sparse, _ = jax.lax.scan(step, jnp.zeros((M, H), jnp.float32), (w13, w2, cw.T))
        return (shared + sparse).reshape(orig_shape)
    x = L0_attn_query
    xn = _layernorm(x, axis=-1)
    x = x + _L0_attn_ref(xn, L0_attn_w_q, L0_attn_b_q, L0_attn_w_k, L0_attn_b_k, L0_attn_w_v, L0_attn_b_v, L0_attn_w_o, L0_attn_b_o) + _L0_ffn_ref(xn, L0_ffn_gate_w, L0_ffn_shared_gate_w, L0_ffn_w13, L0_ffn_w2, L0_ffn_se_gate_up_w, L0_ffn_se_down_w)
    return x

_drawn_inputs = setup_inputs


def setup_inputs(seed=0):
    import zlib

    import numpy as np

    out = dict(_drawn_inputs(seed))
    spreads = {'L0_attn_b_q': (0.0, 2.0),
     'L0_attn_b_k': (0.0, 2.0),
     'L0_attn_b_v': (0.0, 2.0),
     'L0_attn_b_o': (0.0, 0.42)}
    factors = {'L0_attn_w_q': 200.0,
     'L0_attn_w_k': 187.139,
     'L0_attn_w_v': 189.397,
     'L0_attn_w_o': 8.0,
     'L0_ffn_gate_w': 8.0,
     'L0_ffn_shared_gate_w': 8.0,
     'L0_ffn_w13': 8.0,
     'L0_ffn_w2': 8.0,
     'L0_ffn_se_gate_up_w': 4.03,
     'L0_ffn_se_down_w': 4.037}
    for name, (base, spread) in spreads.items():
        noise = np.random.default_rng([zlib.crc32(name.encode()), seed]).standard_normal(out[name].shape)
        drawn = base * np.exp(spread * noise) if base else spread * noise
        out[name] = jnp.asarray(drawn.astype(out[name].dtype))
    for name, factor in factors.items():
        out[name] = (out[name] * factor).astype(out[name].dtype)
    return out
```

```python
from contextlib import ExitStack

import concourse.bass as bass
from concourse import mybir

F32 = mybir.dt.float32
F32R = mybir.dt.float32r
BF16 = mybir.dt.bfloat16
I32 = mybir.dt.int32
U32 = mybir.dt.uint32
ALU = mybir.AluOpType
ACT = mybir.ActivationFunctionType
AX = mybir.AxisListType

P = 128
BATCH, SEQ, D = 2, 512, 256
TOK = BATCH * SEQ
TT = TOK // P
QT = SEQ // P
HC = D // P
NH, HD = 16, 128
UNITS = BATCH * NH
E, TOPK, I = 60, 4, 176
IH = I // 2
SHARED = 4
SCALE = float(HD) ** -0.5
MASKED = -1e10
EPS = 1e-5
TILES = (TOK * TOPK + E * (P - 1)) // P
RING = 8
ZERO_PARTS = 16
ROUND = 1.5 * 2 ** 23

P_AT = (0, P, 3 * P, 6 * P)
PCOLS = 10 * P
PT_AT = {0: 0, 3: 4 * P, 1: 6 * P, 2: 9 * P}
PT_COLS = 11 * P
PT_FROM = (0, P, 2 * P, 2 * P)
SCORES = ((0, 0, 0, 2 * P), (1, 0, 2 * P, 2 * P), (2, 1, 0, 3 * P), (3, 2, 0, 4 * P))
TRANSPOSED = ((1, 0, PT_AT[2], 2 * P), (3, 0, PT_AT[0], 4 * P), (4, 0, PT_AT[3] + P, 4 * P))
PASSES = ((1, 0), (0, 1), (0, 0))
HI, LO = 0, 1


def due(count):
    return not isinstance(count, int) or count > 0


def loads_of(i, j, ahead):
    if isinstance(i, int):
        return 16 * ((i + ahead) // RING + 1)
    return 16 * ((j + ahead) // RING + 1) + (i - j) * (16 // RING)


def layer_kernel(nc, x, w_qk, w_v, w_o, b_v, b_o, gates, w_up, w_down, out):
    with ExitStack() as ctx:
        def sb(name, shape, dt=F32):
            return ctx.enter_context(nc.sbuf_tensor(name, shape, dt))

        def sem(name):
            return ctx.enter_context(nc.semaphore(name))

        x_slots = nc.dram_tensor("x_slots", [TILES * P, D], F32)
        y_slots = nc.dram_tensor("y_slots", [TILES * P, D], F32)

        banks = [ctx.enter_context(nc.psum_tensor(f"bank{k}", [P, 512], F32)) for k in range(8)]

        ident = sb("ident", [P, P])
        identb = sb("identb", [P, P], BF16)
        maskb = sb("maskb", [P, P], BF16)
        acc = sb("acc", [P, TT, D])
        moe = sb("moe", [P, TT, D])
        xnT = moe[:, :, :].rearrange("p t d -> p (t d)").rearrange("p (c n) -> p c n", c=HC)
        xnT_r = sb("xnT_r", [P, 2, HC, TOK], F32R)
        top = sb("top", [P, TT, 8])
        slot = sb("slot", [P, TOPK, TT], I32)
        y_sb = sb("y_sb", [P, RING, D])
        got = sb("got", [P, 4, D])
        part = sb("part", [P, D])
        wqk_in = sb("wqk_in", [P, 2, 2 * HC * HD + 2])
        wv_in = sb("wv_in", [P, HC * 2 * HD])
        wo_in = sb("wo_in", [P, 2, D])
        bias_qk = sb("bias_qk", [P, 2, 2])
        wqk_r = sb("wqk_r", [P, 2, 2, 2 * HC * HD], F32R)
        wv_r = sb("wv_r", [P, 2, HC * 2 * HD], F32R)
        wo_r = sb("wo_r", [P, 2, 2, D], F32R)
        nmax = sb("nmax", [P, 2, QT])
        nmaxs = sb("nmaxs", [P, 2, QT])
        sums = sb("sums", [P, 2, QT])
        rsum = sb("rsum", [P, 2, QT])

        early = ExitStack()

        def sb1(name, shape, dt=F32):
            return early.enter_context(nc.sbuf_tensor(name, shape, dt))

        earlier = sb1("earlier", [P, P], BF16)
        upto = sb1("upto", [P, P], BF16)
        onesb = sb1("onesb", [P, P], BF16)
        iota_e = sb1("iota_e", [P, E])
        iota_p = sb1("iota_p", [P, 1])
        zeros = sb1("zeros", [P, TILES * D // ZERO_PARTS])
        xn = sb1("xn", [P, TT, D])
        bo_sb = sb1("bo_sb", [P, D])
        bvT = sb1("bvT", [P, NH])
        stats = sb1("stats", [P, TT, 6])
        mv = sb1("mv", [P, TT, 2])
        rstd = sb1("rstd", [P, TT])
        vareps = sb1("vareps", [P, TT])
        root = sb1("root", [P, TT])
        gates_sb = sb1("gates_sb", [P, HC, E + 1])
        lmax = sb1("lmax", [P, TT])
        shifted = sb1("shifted", [P, TT, E])
        probs = sb1("probs", [P, TT, E])
        psum_e = sb1("psum_e", [P, TT])
        topi = sb1("topi", [P, TT, 8], U32)
        topf = sb1("topf", [P, TT, 8])
        onehot = sb1("onehot", [P, TOPK, TT, E])
        pair = sb1("pair", [P, 2, TT, E])
        chosen = sb1("chosen", [P, TT, E], BF16)
        ntile = sb1("ntile", [E, P])
        ntileb = sb1("ntileb", [E, P], BF16)
        ends = sb1("ends", [P, E])
        base = sb1("base", [P, E])
        place = sb1("place", [P, TT, E])
        slotf = sb1("slotf", [P, TOPK, TT])
        owner = sb1("owner", [P, 1])
        ownerb = sb1("ownerb", [P, 1], BF16)
        owners = sb1("owners", [1, P], I32)
        sgate = sb1("sgate", [P, TT])
        wup_r = sb1("wup_r", [P, 2, SHARED, HC * 2 * I], F32R)
        wdn_r = sb1("wdn_r", [IH, 2, SHARED, 2 * D], F32R)
        x_t = sb1("x_t", [P, RING, D])
        wup = sb1("wup", [P, RING, HC * 2 * I])
        wdn = sb1("wdn", [IH, RING, 2 * D])
        xT_r = sb1("xT_r", [P, 2, 2, HC * P], F32R)
        sil = sb1("sil", [P, 2, I])
        hid = sb1("hid", [P, 2, I])
        hT_r = sb1("hT_r", [IH, 2, 2, 2 * P], F32R)
        assert NH // 2 == RING and RING % SHARED == 0
        early.close()

        qT_r = sb("qT_r", [P, 2, SEQ], F32R)
        kT_r = sb("kT_r", [P, 2, SEQ], F32R)
        v_r = sb("v_r", [P, 2, 2, QT, 2 * HD], F32R)
        prob = sb("prob", [P, PCOLS])
        probT_r = sb("probT_r", [P, 2, PT_COLS], F32R)
        oT_r = sb("oT_r", [P, 2, SEQ], F32R)

        def value(ap):
            return ap.bitcast(F32)

        ld_x, ld_gates, ld_bias = sem("ld_x"), sem("ld_gates"), sem("ld_bias")
        ld_shared = [sem(f"ld_shared{k}") for k in range(SHARED)]
        zeroed, scattered, out_st = sem("zeroed"), sem("scattered"), sem("out_st")
        ld_xt, ld_up, ld_dn = ([sem(f"ld_{n}{k}") for k in range(RING)] for n in ("xt", "up", "dn"))
        y_st = [sem(f"y_st{k}") for k in range(RING)]
        fetched = [sem(f"fetched{k}") for k in range(4)]
        ld_qk = [sem(f"ld_qk{k}") for k in range(2)]
        ld_o = [sem(f"ld_o{k}") for k in range(2)]
        ld_v, ld_wo_all = sem("ld_v"), [sem(f"ld_wo_all{k}") for k in range(2)]
        split_qk = [sem(f"split_qk{k}") for k in range(2)]
        split_o = [sem(f"split_o{k}") for k in range(2)]
        split_v, split_hi, bias_cp = sem("split_v"), sem("split_hi"), sem("bias_cp")
        split_sh, split_sh_hi = sem("split_sh"), sem("split_sh_hi")
        const0, const1, const2 = sem("const0"), sem("const1"), sem("const2")
        dve_chain, xn_rdy = sem("dve_chain"), sem("xn_rdy")
        var_rdy, root_rdy = sem("var_rdy"), sem("root_rdy")
        bias_ps, xnT_hi, xnT_lo = sem("bias_ps"), sem("xnT_hi"), sem("xnT_lo")
        xnT_ps, xnT_rdy, acc_init = sem("xnT_ps"), sem("xnT_rdy"), sem("acc_init")
        gate_ps, sg_exp = sem("gate_ps"), sem("sg_exp")
        rt_shift, rt_exp, rt_chosen, rt_ntile, rt_owner = (
            sem("rt_" + n) for n in ("shift", "exp", "chosen", "ntile", "owner"))
        count_ps, start_ps, owner_ps = sem("count_ps"), sem("start_ps"), sem("owner_ps")
        slots_rdy, owners_rdy = sem("slots_rdy"), sem("owners_rdy")
        s_h, s_sil, s_hid, s_hTp, s_hTh, s_hT, s_y, s_acc = (
            sem("s_" + n) for n in ("h", "sil", "hid", "hTp", "hTh", "hT", "y", "acc"))
        e_xTp, e_xTh, e_xT, e_h, e_sil, e_hid, e_hTp, e_hTh, e_hT, e_y, e_yc, e_uph, e_up, e_dnh, e_dn = (
            sem("e_" + n) for n in ("xTp", "xTh", "xT", "h", "sil", "hid", "hTp", "hTh", "hT", "y", "yc",
                                    "uph", "up", "dnh", "dn"))
        scaled, summed = sem("scaled"), sem("summed")
        a_q, a_k, a_v, a_qh, a_kh, a_vh, a_qs, a_ks, a_vs = (
            sem("a_" + n) for n in ("q", "k", "v", "qh", "kh", "vh", "qs", "ks", "vs"))
        a_s, a_mx, a_max, a_exp, a_tp, a_pth, a_pt, a_pv, a_oth, a_ot = (
            sem("a_" + n) for n in ("s", "mx", "max", "exp", "tp", "pth", "pt", "pv", "oth", "ot"))
        a_rs, a_out, a_acc, pad_rdy = sem("a_rs"), sem("a_out"), sem("a_acc"), sem("pad_rdy")
        total = sem("total")

        block = ctx.enter_context(nc.Block())

        @block.sync
        def _(sp):
            sp.dma_start(acc[:, :, :], x.rearrange("(t p) d -> p t d", p=P)).then_inc(ld_x, 16)
            sp.dma_start(bvT[:, :], b_v).then_inc(ld_bias, 16)
            sp.dma_start(bo_sb[:, :], b_o.to_broadcast([P, D])).then_inc(ld_bias, 16)
            for g, buffer in enumerate((x_t, y_sb)):
                sp.dma_start(buffer[:, :, :], w_o[g * RING:(g + 1) * RING].rearrange("h p n -> p h n")).then_inc(ld_wo_all[g], 16)
            sp.dma_start(gates_sb[:, :, :], gates).then_inc(ld_gates, 16)
            for q in range(SHARED):
                sp.dma_start(wup[:, q, :], w_up[E + q]).then_inc(ld_shared[q], 16)
                sp.dma_start(wdn[:, q, :], w_down[E + q]).then_inc(ld_shared[q], 16)
            sp.wait_ge(const0, 1)
            flat = x_slots.rearrange("(p r) d -> p (r d)", p=P)
            width = TILES * D // ZERO_PARTS
            for k in range(ZERO_PARTS):
                sp.dma_start(flat[:, k * width:(k + 1) * width], zeros[:, :]).then_inc(zeroed, 16)
            def load_weights(i, k):
                e = sp.value_load(owners[0:1, bass.ds(i, 1)], min_val=0, max_val=E - 1)
                if due(i - RING + 1):
                    sp.wait_ge(e_up, i - RING + 1)
                sp.dma_start(wup[:, k, :], w_up[bass.ds(e, 1)].rearrange("s p n -> p (s n)")).then_inc(ld_up[k], 16)
                if due(i - RING + 1):
                    sp.wait_ge(e_dn, i - RING + 1)
                sp.dma_start(wdn[:, k, :], w_down[bass.ds(e, 1)].rearrange("s p n -> p (s n)")).then_inc(ld_dn[k], 16)

            sp.wait_ge(split_sh, SHARED)
            sp.wait_ge(owners_rdy, 1)
            for i in range(RING):
                load_weights(i, i)
            sp.wait_ge(bias_ps, 1)
            sp.wait_ge(scattered, 16 * TOPK * TT)
            for k in range(RING):
                sp.dma_start(x_t[:, k, :], x_slots[k * P:(k + 1) * P, :]).then_inc(ld_xt[k], 16)
            with sp.Fori(1, TILES // RING) as n:
                for k in range(RING):
                    load_weights(n * RING + k, k)
            for i in range(TILES // RING * RING, TILES):
                load_weights(i, i % RING)

            def load_pair(n):
                for h in range(2):
                    if due(n):
                        sp.wait_ge(split_qk[h], n)
                    sp.dma_start(wqk_in[:, h, :], w_qk[bass.ds(2 * n + h, 1)].rearrange("s p n -> p (s n)")).then_inc(ld_qk[h], 16)
                if due(n):
                    sp.wait_ge(split_v, n)
                sp.dma_start(wv_in[:, :], w_v[bass.ds(n, 1)].rearrange("s p n -> p (s n)")).then_inc(ld_v, 16)
                for h in range(2):
                    if due(n):
                        sp.wait_ge(split_o[h], n)
                    sp.dma_start(wo_in[:, h, :], w_o[bass.ds(2 * n + h, 1)].rearrange("s p n -> p (s n)")).then_inc(ld_o[h], 16)

            load_pair(0)
            with sp.Fori(1, NH // 2) as n:
                load_pair(n)
            for t in range(TT):
                sp.wait_ge(total, t + 1)
                sp.dma_start(out[t * P:(t + 1) * P, :], acc[:, t, :]).then_inc(out_st, 16)
            sp.wait_ge(out_st, 16 * TT)

        def combine(pool, n):
            t, j = divmod(n, TOPK)
            weight = top[:, t, j:j + 1]
            sums_before = (TOPK - 1) * t + max(j - 1, 0)
            pool.wait_ge(fetched[n % 4], 16 * (n // 4 + 1))
            if due(sums_before):
                pool.wait_ge(summed, sums_before)
            into = moe[:, t, :] if j == 0 else part[:, :]
            pool.tensor_scalar(into, got[:, n % 4, :], weight, None, ALU.mult).then_inc(scaled, 1)
            if j:
                pool.wait_ge(scaled, n + 1)
                pool.tensor_tensor(moe[:, t, :], moe[:, t, :], part[:, :], ALU.add).then_inc(summed, 1)

        @block.gpsimd
        def _(pool):
            pool.memset(zeros[:, :], 0.0).then_inc(const0, 1)
            pool.memset(ident[:, :], 0.0).then_inc(const1, 1)
            pool.memset(identb[:, :], 0.0).then_inc(const1, 1)
            pool.memset(maskb[:, :], 0.0).then_inc(const1, 1)
            pool.memset(earlier[:, :], 1.0).then_inc(const1, 1)
            pool.memset(upto[:, :], 1.0).then_inc(const1, 1)
            pool.memset(onesb[:, :], 1.0).then_inc(const1, 1)
            pool.wait_ge(const1, 6)
            for m in (ident, identb):
                pool.affine_select(out=m[:, :], in_=m[:, :], compare_op=ALU.not_equal, fill=1.0,
                                   base=0, pattern=[[-1, P]], channel_multiplier=1).then_inc(const2, 1)
            pool.affine_select(out=maskb[:, :], in_=maskb[:, :], compare_op=ALU.is_ge, fill=MASKED / SCALE,
                               base=0, pattern=[[-1, P]], channel_multiplier=1).then_inc(const2, 1)
            pool.affine_select(out=earlier[:, :], in_=earlier[:, :], compare_op=ALU.is_ge, fill=0.0,
                               base=-1, pattern=[[1, P]], channel_multiplier=-1).then_inc(const2, 1)
            pool.affine_select(out=upto[:, :], in_=upto[:, :], compare_op=ALU.is_ge, fill=0.0,
                               base=0, pattern=[[1, P]], channel_multiplier=-1).then_inc(const2, 1)
            pool.iota(iota_e[:, :], pattern=[[1, E]], base=0, channel_multiplier=0, allow_small_or_imprecise_dtypes=True).then_inc(const2, 1)
            pool.iota(iota_p[:, :], pattern=[[1, 1]], base=0, channel_multiplier=1, allow_small_or_imprecise_dtypes=True).then_inc(const2, 1)
            for q in range(SHARED):
                pool.wait_ge(ld_shared[q], 32)
                pool.tensor_copy(wup_r[:, HI, q, :], wup[:, q, :]).then_inc(split_sh_hi, 1)
                pool.tensor_copy(wdn_r[:, HI, q, :], wdn[:, q, :]).then_inc(split_sh_hi, 1)
                pool.wait_ge(split_sh_hi, 2 * q + 2)
                pool.tensor_tensor(wup_r[:, LO, q, :], wup[:, q, :], value(wup_r[:, HI, q, :]), ALU.subtract)
                pool.tensor_tensor(wdn_r[:, LO, q, :], wdn[:, q, :], value(wdn_r[:, HI, q, :]), ALU.subtract).then_inc(split_sh, 1)
            pool.wait_ge(zeroed, 16 * ZERO_PARTS)
            for j in range(TOPK):
                pool.wait_ge(slots_rdy, j + 1)
                for t in range(TT):
                    pool.indirect_dma_start(
                        out=x_slots[:, :], out_offset=bass.IndirectOffsetOnAxis(ap=slot[:, j, t:t + 1], axis=0),
                        in_=xn[:, t, :], in_offset=None).then_inc(scattered, 16)

            def e_step(i, j):
                if exists(i + 4, TILES):
                    w = (j + 4) % SHARED
                    pool.wait_ge(e_uph, i + 5)
                    pool.tensor_tensor(wup_r[:, LO, w, :], wup[:, (j + 4) % RING, :], value(wup_r[:, HI, w, :]),
                                       ALU.subtract).then_inc(e_up, 1)

            run_tiles(pool, e_step)

            def split(source, hi, lo, n, done):
                pool.tensor_copy(hi, source).then_inc(split_hi, 1)
                pool.wait_ge(split_hi, n + 1)
                pool.tensor_tensor(lo, source, value(hi), ALU.subtract).then_inc(done, 1)

            for n in range(NH // 2):
                for h in range(2):
                    pool.wait_ge(ld_qk[h], 16 * n + 16)
                    if due(n):
                        pool.wait_ge(a_k, 4 * n - 1 + h)
                        pool.wait_ge(a_qs, 4 * n - 1 + h)
                        pool.wait_ge(a_ks, 4 * n - 1 + h)
                    pool.tensor_copy(bias_qk[:, h, :], wqk_in[:, h, 4 * HD:4 * HD + 2]).then_inc(bias_cp, 1)
                    split(wqk_in[:, h, 0:4 * HD], wqk_r[:, h, HI, :], wqk_r[:, h, LO, :], 5 * n + 2 * h, split_qk[h])
                    if h == 0:
                        pool.wait_ge(ld_v, 16 * n + 16)
                        if due(n):
                            pool.wait_ge(a_v, 4 * n)
                        split(wv_in[:, :], wv_r[:, HI, :], wv_r[:, LO, :], 5 * n + 1, split_v)
                for h in range(2):
                    pool.wait_ge(ld_o[h], 16 * n + 16)
                    if due(n):
                        pool.wait_ge(a_out, 2 * (4 * n - 1 + h))
                    split(wo_in[:, h, :], wo_r[:, h, HI, :], wo_r[:, h, LO, :], 5 * n + 3 + h, split_o[h])
                if n == 0:
                    for k in range(RING):
                        pool.wait_ge(y_st[k], 16 * ((TILES - 1 - k) // RING + 1))
                for j in range(TOPK):
                    if due(n):
                        pool.wait_ge(scaled, TOPK * (n - 1) + j + 1)
                    pool.indirect_dma_start(
                        out=got[:, j, :], out_offset=None, in_=y_slots[:, :],
                        in_offset=bass.IndirectOffsetOnAxis(ap=slot[:, j, n:n + 1], axis=0)).then_inc(fetched[j], 16)
                for j in range(TOPK):
                    combine(pool, TOPK * n + j)

        @block.tensor
        def _(pe):
            def three(out_, stationary, moving, first=True, last=True):
                for m, (a, b) in enumerate(PASSES):
                    ins = pe.matmul(out_, stationary(a), moving(b), start=first and m == 0, stop=last and m == 2)
                return ins

            pe.wait_ge(ld_bias, 32)
            for h in range(NH):
                g, k = divmod(h, RING)
                if k == 0:
                    pe.wait_ge(ld_wo_all[g], 16)
                ins = pe.matmul(banks[7][:, 0:D], bvT[:, h:h + 1].to_broadcast([P, P]), (x_t, y_sb)[g][:, k, :],
                                start=h == 0, stop=h == NH - 1)
            ins.then_inc(bias_ps, 1)
            pe.wait_ge(const2, 7)
            for n in range(2 * HC):
                c, g = n % HC, n // HC
                for m in range(4):
                    t = 4 * g + m
                    pe.wait_ge(xn_rdy, t + 1)
                    ins = pe.transpose(banks[n][:, m * P:(m + 1) * P], xn[:, t, c * P:(c + 1) * P], ident[:, :])
                ins.then_inc(xnT_ps, 1)
            pe.wait_ge(xnT_rdy, 4)
            pe.wait_ge(ld_gates, 16)
            for t in range(TT):
                for c in range(HC):
                    ins = pe.matmul(banks[4][:, t * 64:t * 64 + E + 1], xnT[:, c, t * P:(t + 1) * P],
                                    gates_sb[:, c, :], start=c == 0, stop=c == HC - 1)
            ins.then_inc(gate_ps, 1)

            def ranks():
                pe.wait_ge(rt_chosen, 1)
                pe.wait_ge(sg_exp, 1)
                for t in range(TT):
                    for s in range(t + 1):
                        pe.matmul(banks[5][:, t * E:(t + 1) * E], (earlier if s == t else onesb)[:, :],
                                  chosen[:, s, :], start=s == 0, stop=s == t)
                for t in range(TT):
                    ins = pe.matmul(banks[4][0:E, 0:P], chosen[:, t, :], onesb[:, :], start=t == 0, stop=t == TT - 1)
                ins.then_inc(count_ps, 1)

            def starts():
                pe.wait_ge(rt_ntile, 1)
                pe.matmul(banks[4][:, 0:E], ntileb[:, :], earlier[0:E, 0:E], start=True, stop=True)
                pe.matmul(banks[4][:, 64:64 + E], ntileb[:, :], upto[0:E, 0:E], start=True, stop=True).then_inc(start_ps, 1)

            def owner_row():
                pe.wait_ge(rt_owner, 1)
                pe.matmul(banks[4][0:1, 0:P], ownerb[:, :], identb[:, :], start=True, stop=True).then_inc(owner_ps, 1)

            last = SHARED * TT - 1

            def s_step(k, q, t):
                if isinstance(k, int) and k == 4:
                    ranks()
                if isinstance(k, int) and k == 5:
                    starts()
                if isinstance(k, int) and k == 6:
                    owner_row()
                if exists(k + 1, last + 1):
                    q1, t1 = (q + 1, 0) if t == TT - 1 else (q, t + 1)
                    if t1 == 0:
                        pe.wait_ge(split_sh, q1 + 1)
                    if due(k):
                        pe.wait_ge(s_sil, k)
                        pe.wait_ge(s_hid, k)
                    for c in range(HC):
                        ins = three(banks[t1 % 2][:, 0:2 * I], lambda a: xnT_r[:, a, c, t1 * P:(t1 + 1) * P],
                                    lambda a: wup_r[:, a, bass.ds(q1, 1), c * 2 * I:(c + 1) * 2 * I].rearrange("p a n -> p (a n)"),
                                    c == 0, c == HC - 1)
                    ins.then_inc(s_h, 1)
                if exists(k, last + 1):
                    pe.wait_ge(s_hid, k + 1)
                    if due(k - 1):
                        pe.wait_ge(s_hT, k - 1)
                    for c in range(2):
                        ins = pe.transpose(banks[2 + t % 2][0:IH, c * P:(c + 1) * P],
                                           hid[:, t % 2, c * IH:(c + 1) * IH], ident[:, :])
                    ins.then_inc(s_hTp, 1)
                if exists(k - 1, last + 1):
                    q0, t0 = (q - 1, TT - 1) if t == 0 else (q, t - 1)
                    pe.wait_ge(s_hT, k)
                    if due(k - 2):
                        pe.wait_ge(s_acc, k - 2)
                    for c in range(2):
                        ins = three(banks[6 + t0 % 2][:, 0:D], lambda a: hT_r[:, t0 % 2, a, c * P:(c + 1) * P],
                                    lambda a: wdn_r[:, a, bass.ds(q0, 1), c * D:(c + 1) * D].rearrange("p a n -> p (a n)"),
                                    c == 0, c == 1)
                    ins.then_inc(s_y, 1)

            pe.wait_ge(xnT_lo, 4)
            pe.wait_ge(acc_init, 1)
            run_shared(pe, s_step)

            pe.wait_ge(s_acc, last + 1)
            pe.wait_ge(slots_rdy, 1)

            def e_step(i, j):
                if exists(i + 1, TILES):
                    w, b = (j + 1) % SHARED, (j + 1) % 2
                    pe.wait_ge(e_xT, i + 2)
                    pe.wait_ge(e_up, i + 2)
                    if due(i):
                        pe.wait_ge(e_sil, i)
                        pe.wait_ge(e_hid, i)
                    for c in range(HC):
                        ins = three(banks[b][:, 0:2 * I], lambda a: xT_r[:, b, a, c * P:(c + 1) * P],
                                    lambda a: wup_r[:, a, w, c * 2 * I:(c + 1) * 2 * I], c == 0, c == HC - 1)
                    ins.then_inc(e_h, 1)
                if exists(i, TILES):
                    pe.wait_ge(e_hid, i + 1)
                    if due(i - 1):
                        pe.wait_ge(e_hT, i - 1)
                    for c in range(2):
                        ins = pe.transpose(banks[2 + j % 2][0:IH, c * P:(c + 1) * P],
                                           hid[:, j % 2, c * IH:(c + 1) * IH], ident[:, :])
                    ins.then_inc(e_hTp, 1)
                if exists(i + 3, TILES):
                    k, b = (j + 3) % RING, (j + 3) % 2
                    pe.wait_ge(ld_xt[k], loads_of(i, j, 3))
                    if due(i + 2):
                        pe.wait_ge(e_xT, i + 2)
                    for c in range(HC):
                        ins = pe.transpose(banks[4 + b][:, c * P:(c + 1) * P], x_t[:, k, c * P:(c + 1) * P], ident[:, :])
                    ins.then_inc(e_xTp, 1)
                if exists(i - 1, TILES):
                    w, b = (j - 1) % SHARED, (j - 1) % 2
                    pe.wait_ge(e_hT, i)
                    pe.wait_ge(e_dn, i)
                    if due(i - 2):
                        pe.wait_ge(e_yc, i - 2)
                    for c in range(2):
                        ins = three(banks[6 + b][:, 0:D], lambda a: hT_r[:, b, a, c * P:(c + 1) * P],
                                    lambda a: wdn_r[:, a, w, c * D:(c + 1) * D], c == 0, c == 1)
                    ins.then_inc(e_y, 1)

            run_tiles(pe, e_step)

            pe.wait_ge(e_yc, TILES)

            def project(u, j, n):
                h, b = j % 2, j // 2
                pe.wait_ge(split_qk[h], n + 1)
                for which, done in ((0, a_q), (1, a_k)):
                    if isinstance(u, int) and u == 1:
                        pe.wait_ge(a_vs, 1 + which)
                    elif isinstance(u, int) and u == 2:
                        pe.wait_ge((a_qs, a_ks)[which], 2)
                    elif due(u):
                        pe.wait_ge(a_acc, 2 * (u - 3) + 1 + which)
                    for c in range(HC):
                        at = (which * HC + c) * HD
                        ins = three(banks[6 + which][:, :], lambda a: wqk_r[:, h, a, at:at + HD],
                                    lambda a: xnT_r[:, a, c, b * SEQ:(b + 1) * SEQ], c == 0, c == HC - 1)
                    ins.then_inc(done, 1)
                if h == 0:
                    pe.wait_ge(split_v, n + 1)
                    for g in range(2):
                        pe.wait_ge((a_qs, a_ks)[g], u + 1)
                        for m in range(2):
                            t = b * QT + 2 * g + m
                            for c in range(HC):
                                ins = three(banks[6 + g][:, m * 2 * HD:(m + 1) * 2 * HD],
                                            lambda a: xnT_r[:, a, c, t * P:(t + 1) * P],
                                            lambda a: wv_r[:, a, c * 2 * HD:(c + 1) * 2 * HD], c == 0, c == HC - 1)
                        ins.then_inc(a_v, 1)

            def scores(u):
                pe.wait_ge(a_qs, u + 1)
                pe.wait_ge(a_ks, u + 1)
                if due(u):
                    pe.wait_ge(a_exp, 3 * u)
                    pe.wait_ge(a_pt, 3 * u - 2)
                for q, bank, at, keys in SCORES:
                    three(banks[bank][:, at:at + keys], lambda a: qT_r[:, a, q * P:(q + 1) * P],
                          lambda a: kT_r[:, a, 0:keys], last=False)
                    ins = pe.matmul(banks[bank][:, at + q * P:at + (q + 1) * P], identb[:, :], maskb[:, :],
                                    start=False, stop=True)
                    if q:
                        ins.then_inc(a_s, 1)

            def transposes(u):
                pe.wait_ge(a_exp, 3 * u + 3)
                if due(u):
                    pe.wait_ge(a_pt, 3 * u)
                for bank, keys in ((1, (2,)), (3, (0,)), (4, (3, 1))):
                    at = 0
                    for k in keys:
                        for q in range(k, QT):
                            ins = pe.transpose(banks[bank][:, at:at + P],
                                               prob[:, P_AT[q] + k * P:P_AT[q] + (k + 1) * P], ident[:, :])
                            at += P
                    ins.then_inc(a_tp, 1)

            def output(u, j, n):
                h = j % 2
                pe.wait_ge(a_ot, u + 1)
                pe.wait_ge(split_o[h], n + 1)
                for g in range(2):
                    if isinstance(u, int) and u + 2 >= UNITS:
                        pe.wait_ge(a_acc, 2 * u - 1 + g)
                    elif h == 0:
                        pe.wait_ge(a_vs, u + 3 + g)
                    else:
                        pe.wait_ge((a_qs, a_ks)[g], u + 3)
                    for m in range(2):
                        q = 2 * g + m
                        ins = three(banks[6 + g][:, m * D:(m + 1) * D], lambda a: oT_r[:, a, q * P:(q + 1) * P],
                                    lambda a: wo_r[:, h, a, :])
                    ins.then_inc(a_out, 1)

            def weigh(u, j):
                h, b = j % 2, j // 2
                pe.wait_ge(a_pt, 3 * u + 3)
                pe.wait_ge(a_vs, u + 2 - h)
                if due(u):
                    pe.wait_ge(a_ot, u)
                else:
                    pe.wait_ge(pad_rdy, 1)
                for k in range(QT):
                    cols = SEQ - PT_FROM[k]
                    ins = three(banks[5][:, PT_FROM[k]:SEQ], lambda a: v_r[:, a, b, k, h * HD:(h + 1) * HD],
                                lambda a: probT_r[:, a, PT_AT[k]:PT_AT[k] + cols], k == 0, k == QT - 1)
                ins.then_inc(a_pv, 1)

            def a_step(u, j, n):
                if exists(u + 1, UNITS):
                    project(u + 1, (j + 1) % 4, n + (j == 3))
                if exists(u, UNITS):
                    transposes(u)
                if exists(u - 1, UNITS):
                    output(u - 1, (j - 1) % 4, n - (j == 0))
                if exists(u + 1, UNITS):
                    scores(u + 1)
                if exists(u, UNITS):
                    weigh(u, j)

            run_units(pe, a_step)

        @block.scalar
        def _(act):
            act.wait_ge(var_rdy, 1)
            act.activation(root[:, :], vareps[:, :], ACT.Sqrt).then_inc(root_rdy, 1)
            for n in range(2 * HC):
                c, g = n % HC, n // HC
                act.wait_ge(xnT_ps, n + 1)
                cols = slice(g * 4 * P, (g + 1) * 4 * P)
                act.activation(xnT[:, c, cols], banks[n][:, :], ACT.Copy).then_inc(xnT_rdy, 1)
                act.activation(xnT_r[:, HI, c, cols], banks[n][:, :], ACT.Copy).then_inc(xnT_hi, 1)
            act.wait_ge(rt_shift, 1)
            act.activation(probs[:, :, :], shifted[:, :, :], ACT.Exp).then_inc(rt_exp, 1)
            logits = banks[4][:, :].rearrange("p (t e) -> p t e", e=64)
            act.activation(sgate[:, :], logits[:, :, E:E + 1].rearrange("p t a -> p (t a)"), ACT.Exp,
                           scale=-1.0).then_inc(sg_exp, 1)

            def s_step(k, t):
                if exists(k + 1, SHARED * TT):
                    b = (t + 1) % 2
                    act.wait_ge(s_h, k + 2)
                    if due(k):
                        act.wait_ge(s_hid, k)
                    act.activation(sil[:, b, :], banks[b][:, 0:I], ACT.Silu).then_inc(s_sil, 1)
                if exists(k, SHARED * TT):
                    b = t % 2
                    act.wait_ge(s_hTp, k + 1)
                    if due(k - 1):
                        act.wait_ge(s_y, k - 1)
                    act.activation(hT_r[:, b, HI, :], banks[2 + b][0:IH, 0:2 * P], ACT.Copy).then_inc(s_hTh, 1)

            run_shared(act, lambda k, q, t: s_step(k, t))

            def e_step(i, j):
                if exists(i + 1, TILES):
                    b = (j + 1) % 2
                    act.wait_ge(e_h, i + 2)
                    if due(i):
                        act.wait_ge(e_hid, i)
                    act.activation(sil[:, b, :], banks[b][:, 0:I], ACT.Silu).then_inc(e_sil, 1)
                if exists(i, TILES):
                    b = j % 2
                    act.wait_ge(e_hTp, i + 1)
                    if due(i - 1):
                        act.wait_ge(e_y, i - 1)
                    act.activation(hT_r[:, b, HI, :], banks[2 + b][0:IH, 0:2 * P], ACT.Copy).then_inc(e_hTh, 1)
                if exists(i + 3, TILES):
                    b = (j + 3) % 2
                    act.wait_ge(e_xTp, i + 4)
                    if due(i + 2):
                        act.wait_ge(e_h, i + 2)
                    act.activation(xT_r[:, b, HI, :], banks[4 + b][:, 0:HC * P], ACT.Copy).then_inc(e_xTh, 1)
                if exists(i + 3, TILES - RING):
                    k = (j + 3) % RING
                    act.dma_start(x_t[:, k, :], x_slots[bass.ds((i + 3 + RING) * P, P), :]).then_inc(ld_xt[k], 16)
                if exists(i + 4, TILES):
                    k, w = (j + 4) % RING, (j + 4) % SHARED
                    act.wait_ge(ld_up[k], loads_of(i, j, 4))
                    if due(i + 1):
                        act.wait_ge(e_h, i + 1)
                    act.activation(wup_r[:, HI, w, :], wup[:, k, :], ACT.Copy).then_inc(e_uph, 1)
                if exists(i + 2, TILES):
                    k, w = (j + 2) % RING, (j + 2) % SHARED
                    act.wait_ge(ld_dn[k], loads_of(i, j, 2))
                    if due(i - 1):
                        act.wait_ge(e_y, i - 1)
                    act.activation(wdn_r[:, HI, w, :], wdn[:, k, :], ACT.Copy).then_inc(e_dnh, 1)
                if exists(i - 2, TILES):
                    k = (j - 2) % RING
                    act.wait_ge(e_yc, i - 1)
                    act.dma_start(y_slots[bass.ds((i - 2) * P, P), :], y_sb[:, k, :]).then_inc(y_st[k], 16)

            act.wait_ge(s_y, SHARED * TT)
            run_tiles(act, e_step)

            def a_step(u, j, n):
                if exists(u + 1, UNITS):
                    h, b = (j + 1) % 2, ((j + 1) % 4) // 2
                    if due(u + 1):
                        act.wait_ge(a_s, 3 * (u + 1))
                    act.wait_ge(a_q, u + 2)
                    act.activation(qT_r[:, HI, :], banks[6][:, :], ACT.Identity, bias=bias_qk[:, h, 0:1]).then_inc(a_qh, 1)
                    act.wait_ge(a_k, u + 2)
                    act.activation(kT_r[:, HI, :], banks[7][:, :], ACT.Identity, bias=bias_qk[:, h, 1:2]).then_inc(a_kh, 1)
                    if h == 0:
                        if due(u - 1):
                            act.wait_ge(a_pv, u - 1)
                        for g in range(2):
                            act.wait_ge(a_v, u + 2 + g)
                            act.activation(v_r[:, HI, b, 2 * g:2 * g + 2, :].rearrange("p t n -> p (t n)"),
                                           banks[6 + g][:, :], ACT.Copy).then_inc(a_vh, 1)
                if exists(u, UNITS):
                    if due(u):
                        act.wait_ge(a_pv, u)
                    for m, (bank, at, to, cols) in enumerate(TRANSPOSED):
                        act.wait_ge(a_tp, 3 * u + 1 + m)
                        act.activation(probT_r[:, HI, to:to + cols], banks[bank][:, at:at + cols], ACT.Copy).then_inc(a_pth, 1)
                if exists(u + 1, UNITS):
                    b = (j + 1) % 2
                    if due(u + 1):
                        act.wait_ge(a_tp, 3 * (u + 1))
                    act.wait_ge(a_max, u + 2)
                    for q, bank, at, _ in SCORES:
                        keys = (q + 1) * P
                        ins = act.activation(prob[:, P_AT[q]:P_AT[q] + keys], banks[bank][:, at:at + keys], ACT.Exp,
                                             bias=nmaxs[:, b, q:q + 1], scale=SCALE, accum_out=sums[:, b, q:q + 1])
                        if q:
                            ins.then_inc(a_exp, 1)
                if exists(u, UNITS):
                    act.wait_ge(a_pv, u + 1)
                    if due(u):
                        act.wait_ge(a_out, 2 * u)
                    act.activation(oT_r[:, HI, :], banks[5][:, :], ACT.Copy).then_inc(a_oth, 1)

            run_units(act, a_step)

        @block.vector
        def _(dve):
            chain = [0]

            def link(ins):
                chain[0] += 1
                ins.then_inc(dve_chain, 1)
                dve.wait_ge(dve_chain, chain[0])

            dve.wait_ge(ld_x, 16)
            for t in range(TT):
                ins = dve.bn_stats(stats[:, t, :], acc[:, t, :])
            link(ins)
            for t in range(TT):
                ins = dve.bn_aggr(mv[:, t, :], stats[:, t, :])
            link(ins)
            dve.tensor_scalar(vareps[:, :], mv[:, :, 1], EPS, None, ALU.add).then_inc(var_rdy, 1)
            dve.wait_ge(root_rdy, 1)
            link(dve.reciprocal(rstd[:, :], root[:, :]))
            link(dve.tensor_tensor(root[:, :], rstd[:, :], rstd[:, :], ALU.mult))
            link(dve.tensor_tensor(root[:, :], root[:, :], vareps[:, :], ALU.mult))
            link(dve.tensor_scalar(root[:, :], root[:, :], -0.5, 1.5, ALU.mult, ALU.add))
            link(dve.tensor_tensor(rstd[:, :], rstd[:, :], root[:, :], ALU.mult))
            for t in range(TT):
                dve.tensor_scalar(xn[:, t, :], acc[:, t, :], mv[:, t, 0:1], rstd[:, t:t + 1],
                                  ALU.subtract, ALU.mult).then_inc(xn_rdy, 1)
            dve.wait_ge(ld_bias, 32)
            for n in range(2 * HC):
                c, g = n % HC, n // HC
                cols = slice(g * 4 * P, (g + 1) * 4 * P)
                dve.wait_ge(xnT_hi, n + 1)
                dve.tensor_tensor(xnT_r[:, LO, c, cols], banks[n][:, :], value(xnT_r[:, HI, c, cols]),
                                  ALU.subtract).then_inc(xnT_lo, 1)

            dve.wait_ge(bias_ps, 1)
            link(dve.tensor_tensor(bo_sb[:, :], bo_sb[:, :], banks[7][:, 0:D], ALU.add))
            dve.tensor_tensor(acc[:, :, :], acc[:, :, :], bo_sb[:, None, :].to_broadcast([P, TT, D]), ALU.add).then_inc(acc_init, 1)

            logits = banks[4][:, :].rearrange("p (t e) -> p t e", e=64)[:, :, 0:E]
            over = [P, TT, E]
            dve.wait_ge(gate_ps, 1)
            dve.wait_ge(const2, 7)
            link(dve.tensor_reduce(lmax[:, :], logits, AX.X, ALU.max))
            dve.tensor_tensor(shifted[:, :, :], logits, lmax[:, :, None].to_broadcast(over), ALU.subtract).then_inc(rt_shift, 1)
            dve.wait_ge(sg_exp, 1)
            link(dve.tensor_scalar(sgate[:, :], sgate[:, :], 1.0, None, ALU.add))
            link(dve.reciprocal(sgate[:, :], sgate[:, :]))
            dve.wait_ge(acc_init, 1)

            def softmax():
                dve.wait_ge(rt_exp, 1)
                link(dve.tensor_reduce(psum_e[:, :], probs[:, :, :], AX.X, ALU.add))
                link(dve.reciprocal(psum_e[:, :], psum_e[:, :]))
                link(dve.tensor_tensor(probs[:, :, :], probs[:, :, :], psum_e[:, :, None].to_broadcast(over), ALU.mult))

            def largest():
                for t in range(TT):
                    ins = dve.max(top[:, t, :], probs[:, t, :])
                link(ins)

            def indices():
                for t in range(TT):
                    ins = dve.max_index(topi[:, t, :], top[:, t, :], probs[:, t, :])
                link(ins)
                link(dve.tensor_copy(topf[:, :, :], topi[:, :, :]))

            def onehots():
                for j in range(TOPK):
                    ins = dve.tensor_tensor(onehot[:, j], iota_e[:, None, :].to_broadcast(over),
                                            topf[:, :, j:j + 1].to_broadcast(over), ALU.is_equal)
                link(ins)

            def choices():
                for j in range(2):
                    ins = dve.tensor_tensor(pair[:, j], onehot[:, 2 * j], onehot[:, 2 * j + 1], ALU.add)
                link(ins)
                dve.tensor_tensor(chosen[:, :, :], pair[:, 0], pair[:, 1], ALU.add).then_inc(rt_chosen, 1)

            def tile_counts():
                dve.wait_ge(count_ps, 1)
                link(dve.tensor_scalar(ntile[:, :], banks[4][0:E, 0:P], float(P - 1), 1.0 / P, ALU.add, ALU.mult))
                link(dve.tensor_scalar(ntile[:, :], ntile[:, :], -(P - 1) / (2.0 * P), ROUND, ALU.add, ALU.add))
                dve.tensor_scalar(ntileb[:, :], ntile[:, :], ROUND, None, ALU.subtract).then_inc(rt_ntile, 1)

            def tile_owners():
                dve.wait_ge(start_ps, 1)
                dve.tensor_scalar(base[:, :], banks[4][:, 0:E], float(P), None, ALU.mult)
                link(dve.tensor_scalar(ends[:, :], banks[4][:, 64:64 + E], iota_p[:, 0:1], None, ALU.is_le))
                link(dve.tensor_reduce(owner[:, :], ends[:, :], AX.X, ALU.add))
                dve.tensor_scalar(ownerb[:, :], owner[:, :], float(E - 1), None, ALU.min).then_inc(rt_owner, 1)
                link(dve.tensor_tensor(place[:, :, :], banks[5][:, 0:TT * E].rearrange("p (t e) -> p t e", e=E),
                                       base[:, None, :].to_broadcast(over), ALU.add))

            def slots_of(choice):
                link(dve.tensor_tensor(pair[:, choice % 2], onehot[:, choice], place[:, :, :], ALU.mult))
                link(dve.tensor_reduce(slotf[:, choice, :], pair[:, choice % 2], AX.X, ALU.add))
                dve.tensor_copy(slot[:, choice, :], slotf[:, choice, :]).then_inc(slots_rdy, 1)

            def routing(k):
                if k == -1:
                    softmax()
                if k == 0:
                    largest()
                if k == 1:
                    indices()
                if k == 2:
                    onehots()
                if k == 3:
                    choices()
                if k == 4:
                    tile_counts()
                if k == 5:
                    tile_owners()
                if k == 6:
                    slots_of(0)
                    dve.wait_ge(owner_ps, 1)
                    dve.tensor_copy(owners[:, :], banks[4][0:1, 0:P]).then_inc(owners_rdy, 1)
                    slots_of(1)
                if k == 7:
                    slots_of(2)
                    slots_of(3)

            def s_step(k, t):
                if exists(k + 1, SHARED * TT):
                    b = (t + 1) % 2
                    dve.wait_ge(s_sil, k + 2)
                    if due(k):
                        dve.wait_ge(s_hTp, k)
                    dve.tensor_tensor(hid[:, b, :], sil[:, b, :], banks[b][:, I:2 * I], ALU.mult).then_inc(s_hid, 1)
                if exists(k - 1, SHARED * TT):
                    b, t0 = (t - 1) % 2, (t - 1) % TT
                    dve.wait_ge(s_y, k)
                    if due(k - 3):
                        dve.wait_ge(s_acc, k - 3)
                    dve.scalar_tensor_tensor(out=acc[:, t0, :], in0=banks[6 + b][:, 0:D], scalar=sgate[:, t0:t0 + 1],
                                             in1=acc[:, t0, :], op0=ALU.mult, op1=ALU.add).then_inc(s_acc, 1)
                if exists(k, SHARED * TT):
                    b = t % 2
                    dve.wait_ge(s_hTh, k + 1)
                    dve.tensor_tensor(hT_r[:, b, LO, :], banks[2 + b][0:IH, 0:2 * P], value(hT_r[:, b, HI, :]),
                                      ALU.subtract).then_inc(s_hT, 1)
                if isinstance(k, int):
                    routing(k)

            run_shared(dve, lambda k, q, t: s_step(k, t))

            def e_step(i, j):
                if exists(i + 1, TILES):
                    b = (j + 1) % 2
                    dve.wait_ge(e_sil, i + 2)
                    if due(i):
                        dve.wait_ge(e_hTp, i)
                    dve.tensor_tensor(hid[:, b, :], sil[:, b, :], banks[b][:, I:2 * I], ALU.mult).then_inc(e_hid, 1)
                if exists(i, TILES):
                    b = j % 2
                    dve.wait_ge(e_hTh, i + 1)
                    dve.tensor_tensor(hT_r[:, b, LO, :], banks[2 + b][0:IH, 0:2 * P], value(hT_r[:, b, HI, :]),
                                      ALU.subtract).then_inc(e_hT, 1)
                if exists(i + 3, TILES):
                    b = (j + 3) % 2
                    dve.wait_ge(e_xTh, i + 4)
                    dve.tensor_tensor(xT_r[:, b, LO, :], banks[4 + b][:, 0:HC * P], value(xT_r[:, b, HI, :]),
                                      ALU.subtract).then_inc(e_xT, 1)
                if exists(i - 1, TILES):
                    b, k = (j - 1) % 2, (j - 1) % RING
                    dve.wait_ge(e_y, i)
                    if isinstance(i, int):
                        if due(16 * ((i - 1) // RING)):
                            dve.wait_ge(y_st[k], 16 * ((i - 1) // RING))
                    else:
                        dve.wait_ge(y_st[k], (i - j) * (16 // RING) - (16 if j == 0 else 0))
                    dve.tensor_copy(y_sb[:, k, :], banks[6 + b][:, 0:D]).then_inc(e_yc, 1)
                if exists(i + 2, TILES):
                    w = (j + 2) % SHARED
                    dve.wait_ge(e_dnh, i + 3)
                    dve.tensor_tensor(wdn_r[:, LO, w, :], wdn[:, (j + 2) % RING, :], value(wdn_r[:, HI, w, :]),
                                      ALU.subtract).then_inc(e_dn, 1)

            run_tiles(dve, e_step)

            for a in (HI, LO):
                ins = dve.memset(value(probT_r[:, a, PT_AT[3]:PT_AT[3] + P]), 0.0)
            ins.then_inc(pad_rdy, 1)

            def a_step(u, j, n):
                if exists(u + 1, UNITS):
                    j1 = (j + 1) % 4
                    h, b = j1 % 2, j1 // 2
                    for which, (hi_done, to, done) in enumerate(((a_qh, qT_r, a_qs), (a_kh, kT_r, a_ks))):
                        dve.wait_ge(hi_done, u + 2)
                        dve.scalar_tensor_tensor(out=to[:, LO, :], in0=banks[6 + which][:, :],
                                                 scalar=bias_qk[:, h, which:which + 1], in1=value(to[:, HI, :]),
                                                 op0=ALU.add, op1=ALU.subtract).then_inc(done, 1)
                    if h == 0:
                        for g in range(2):
                            dve.wait_ge(a_vh, u + 2 + g)
                            tiles = slice(2 * g, 2 * g + 2)
                            dve.tensor_tensor(v_r[:, LO, b, tiles, :], banks[6 + g][:, :].rearrange("p (t n) -> p t n", t=2),
                                              value(v_r[:, HI, b, tiles, :]), ALU.subtract).then_inc(a_vs, 1)
                if exists(u, UNITS):
                    for m, (bank, at, to, cols) in enumerate(TRANSPOSED):
                        dve.wait_ge(a_pth, 3 * u + 1 + m)
                        dve.tensor_tensor(probT_r[:, LO, to:to + cols], banks[bank][:, at:at + cols],
                                          value(probT_r[:, HI, to:to + cols]), ALU.subtract).then_inc(a_pt, 1)
                    dve.wait_ge(a_exp, 3 * u + 3)
                    dve.reciprocal(rsum[:, j % 2, :], sums[:, j % 2, :]).then_inc(a_rs, 1)
                if exists(u - 1, UNITS):
                    j0 = (j - 1) % 4
                    dve.wait_ge(a_rs, u)
                    if due(u - 1):
                        dve.wait_ge(a_acc, 2 * (u - 1))
                    for g in range(2):
                        dve.wait_ge(a_out, 2 * (u - 1) + 1 + g)
                        for m in range(2):
                            q = 2 * g + m
                            to = acc[:, (j0 // 2) * QT + q, :]
                            ins = dve.scalar_tensor_tensor(out=to, in0=banks[6 + g][:, m * D:(m + 1) * D],
                                                           scalar=rsum[:, j0 % 2, q:q + 1], in1=to,
                                                           op0=ALU.mult, op1=ALU.add)
                        ins.then_inc(a_acc, 1)
                if exists(u + 1, UNITS):
                    b = (j + 1) % 2
                    for q, bank, at, _ in SCORES:
                        dve.wait_ge(a_s, 3 * (u + 1) + 1 + bank)
                        ins = dve.tensor_reduce(nmax[:, b, q:q + 1], banks[bank][:, at:at + (q + 1) * P],
                                                AX.X, ALU.max, negate=True)
                    ins.then_inc(a_mx, 1)
                    dve.wait_ge(a_mx, u + 2)
                    dve.tensor_scalar(nmaxs[:, b, :], nmax[:, b, :], SCALE, None, ALU.mult).then_inc(a_max, 1)
                if exists(u, UNITS):
                    dve.wait_ge(a_oth, u + 1)
                    dve.tensor_tensor(oT_r[:, LO, :], banks[5][:, :], value(oT_r[:, HI, :]), ALU.subtract).then_inc(a_ot, 1)

            run_units(dve, a_step)
            dve.wait_ge(summed, (TOPK - 1) * TT)
            dve.wait_ge(a_acc, 2 * UNITS)
            for t in range(TT):
                dve.tensor_tensor(acc[:, t, :], acc[:, t, :], moe[:, t, :], ALU.add).then_inc(total, 1)


def exists(index, count):
    return not isinstance(index, int) or 0 <= index < count


def run_shared(eng, step):
    step(-1, -1, TT - 1)
    for t in range(TT):
        step(t, 0, t)
    with eng.Fori(1, SHARED - 1) as q:
        for t in range(TT):
            step(q * TT + t, q, t)
    for t in range(TT):
        step((SHARED - 1) * TT + t, SHARED - 1, t)
    step(SHARED * TT, SHARED, 0)


def run_tiles(eng, step):
    full = (TILES - 4 - RING) // RING
    for i in range(-4, RING + 1):
        step(i, i % RING)
    with eng.Fori(1, full) as n:
        for i in range(1, RING + 1):
            step(n * RING + i, i % RING)
    for i in range(full * RING + 1, TILES + 2):
        step(i, i % RING)


def run_units(eng, step):
    for u in range(-1, 4):
        step(u, u % 4, u // 4)
    with eng.Fori(1, UNITS // 4 - 1) as n:
        for j in range(4):
            step(n * 4 + j, j, n)
    for u in range(UNITS - 4, UNITS + 1):
        step(u, u % 4, u // 4)


def kernel(L0_attn_query, L0_attn_w_q, L0_attn_b_q, L0_attn_w_k, L0_attn_b_k, L0_attn_w_v, L0_attn_b_v,
           L0_attn_w_o, L0_attn_b_o, L0_ffn_gate_w, L0_ffn_shared_gate_w, L0_ffn_w13, L0_ffn_w2,
           L0_ffn_se_gate_up_w, L0_ffn_se_down_w):
    import numpy as np
    import concourse.bacc as bacc
    from concourse.bass_utils import run_bass_kernel_spmd

    f = np.ascontiguousarray

    def by_head(w):
        return np.asarray(w).reshape(HC, P, NH, HD).transpose(2, 1, 0, 3)

    def column(b):
        return np.asarray(b).reshape(NH, HD, 1)

    w_qk = f(np.concatenate([by_head(L0_attn_w_q).reshape(NH, P, HC * HD), by_head(L0_attn_w_k).reshape(NH, P, HC * HD),
                             column(L0_attn_b_q), column(L0_attn_b_k)], axis=2))
    w_v = f(np.asarray(L0_attn_w_v).reshape(HC, P, NH // 2, 2 * HD).transpose(2, 1, 0, 3).reshape(NH // 2, P, HC * 2 * HD))
    w_o = f(np.asarray(L0_attn_w_o).reshape(NH, HD, D))
    gate_up = np.asarray(L0_ffn_se_gate_up_w).reshape(2, SHARED, I, D).transpose(1, 0, 2, 3).reshape(SHARED, 2 * I, D)
    down = np.asarray(L0_ffn_se_down_w).reshape(D, SHARED, I).transpose(1, 0, 2)
    up_all = np.concatenate([np.asarray(L0_ffn_w13), gate_up])
    down_all = np.concatenate([np.asarray(L0_ffn_w2), down])
    w_up = f(up_all.transpose(0, 2, 1).reshape(E + SHARED, HC, P, 2 * I).transpose(0, 2, 1, 3).reshape(E + SHARED, P, HC * 2 * I))
    w_down = f(down_all.transpose(0, 2, 1).reshape(E + SHARED, 2, IH, D).transpose(0, 2, 1, 3).reshape(E + SHARED, IH, 2 * D))
    gates = f(np.concatenate([np.asarray(L0_ffn_gate_w), np.asarray(L0_ffn_shared_gate_w)]).T.reshape(HC, P, E + 1).transpose(1, 0, 2))
    arrays = {
        "x": f(np.asarray(L0_attn_query).reshape(TOK, D)), "w_qk": w_qk, "w_v": w_v, "w_o": w_o,
        "b_v": f(np.asarray(L0_attn_b_v).reshape(NH, HD).T), "b_o": f(np.asarray(L0_attn_b_o).reshape(1, D)),
        "gates": gates, "w_up": w_up, "w_down": w_down,
    }
    nc = bacc.Bacc("TRN2", target_bir_lowering=False, num_devices=1)
    args = [nc.dram_tensor(name, a.shape, mybir.dt.from_np(a.dtype), kind="ExternalInput").ap() for name, a in arrays.items()]
    out = nc.dram_tensor("out", (TOK, D), F32, kind="ExternalOutput").ap()
    layer_kernel(nc, *args, out)
    r = run_bass_kernel_spmd(nc, [arrays], core_ids=[0])
    return r.results[0]["out"].reshape(BATCH, SEQ, D)
```

```python
from contextlib import ExitStack

import concourse.bass as bass
from concourse import mybir

F32 = mybir.dt.float32
F32R = mybir.dt.float32r
BF16 = mybir.dt.bfloat16
I32 = mybir.dt.int32
U32 = mybir.dt.uint32
ALU = mybir.AluOpType
ACT = mybir.ActivationFunctionType
AX = mybir.AxisListType

P = 128
BATCH, SEQ, D = 2, 512, 256
TOK = BATCH * SEQ
TT = TOK // P
QT = SEQ // P
HC = D // P
NH, HD = 16, 128
UNITS = BATCH * NH
E, TOPK, I = 60, 4, 176
IH = I // 2
SHARED = 4
SCALE = float(HD) ** -0.5
MASKED = -1e10
EPS = 1e-5
TILES = (TOK * TOPK + E * (P - 1)) // P
RING = 12
Y_RING = 12
ZERO_PARTS = 16
EARLY = 3
WARM_UP = 12
BIAS_STEP = 25
ROUND = 1.5 * 2 ** 23

P_AT = (0, P, 3 * P, 6 * P)
PCOLS = 10 * P
PT_AT = {0: 0, 3: 4 * P, 1: 6 * P, 2: 9 * P}
PT_COLS = 11 * P
PT_FROM = (0, P, 2 * P, 2 * P)
SCORES = ((0, 0, 2 * P, 2 * P), (1, 0, 0, 2 * P), (2, 1, 0, 3 * P), (3, 2, 0, 4 * P))
TRANSPOSED = ((1, 0, PT_AT[2], 2 * P), (3, 0, PT_AT[0], 4 * P), (4, 0, PT_AT[3] + P, 4 * P))
PASSES = ((1, 0), (0, 1), (0, 0))
HI, LO = 0, 1


def due(count):
    return not isinstance(count, int) or count > 0


def round_of(j, r, ahead, ring):
    return r * (RING // ring) + (j + ahead) // ring


def layer_kernel(nc, x, w_qk, w_v, w_o, b_v, b_o, gates, w_up, w_down, out):
    with ExitStack() as ctx:
        def sb(name, shape, dt=F32):
            return ctx.enter_context(nc.sbuf_tensor(name, shape, dt))

        def sem(name):
            return ctx.enter_context(nc.semaphore(name))

        x_slots = nc.dram_tensor("x_slots", [TILES * P, D], F32)
        y_slots = nc.dram_tensor("y_slots", [TILES * P, D], F32)

        def tile_rows(slots, i, count):
            return slots[bass.ds(i * P, count * P), :].rearrange("(t p) d -> p t d", p=P)


        banks = [ctx.enter_context(nc.psum_tensor(f"bank{k}", [P, 512], F32)) for k in range(8)]

        ident = sb("ident", [P, P])
        identb = sb("identb", [P, P], BF16)
        maskb = sb("maskb", [P, P], BF16)
        acc = sb("acc", [P, TT, D])
        moe = sb("moe", [P, TT, D])
        xnT = moe[:, :, :].rearrange("p t d -> p (t d)").rearrange("p (c n) -> p c n", c=HC)
        xnT_r = sb("xnT_r", [P, 2, HC, TOK], F32R)
        top = sb("top", [P, TT, 8])
        slot = sb("slot", [P, TOPK, TT], I32)
        y_sb = sb("y_sb", [P, Y_RING, D])
        bias_qk = sb("bias_qk", [P, 2, 2])
        nmax = sb("nmax", [P, 2, QT])
        nmaxs = sb("nmaxs", [P, 2, QT])
        sums = sb("sums", [P, 2, QT])
        rsum = sb("rsum", [P, 2, QT])

        early = ExitStack()

        def sb1(name, shape, dt=F32):
            return early.enter_context(nc.sbuf_tensor(name, shape, dt))

        earlier = sb1("earlier", [P, P], BF16)
        upto = sb1("upto", [P, P], BF16)
        onesb = sb1("onesb", [P, P], BF16)
        iota_e = sb1("iota_e", [P, E], BF16)
        iota_p = sb1("iota_p", [P, 1])
        zeros = sb1("zeros", [P, TILES * D // ZERO_PARTS])
        xn = sb1("xn", [P, TT, D])
        bias_part = sb1("bias_part", [P, D])
        ones = sb1("ones", [P, 1])
        bvT = sb1("bvT", [P, NH])
        stats = sb1("stats", [P, TT, 6])
        mv = sb1("mv", [P, TT, 2])
        rstd = sb1("rstd", [P, TT])
        vareps = sb1("vareps", [P, TT])
        root = sb1("root", [P, TT])
        lmax = sb1("lmax", [P, TT])
        shifted = sb1("shifted", [P, TT, E])
        probs = sb1("probs", [P, TT, E])
        psum_e = sb1("psum_e", [P, TT])
        topi = sb1("topi", [P, TT, 8], U32)
        topb = sb1("topb", [P, TT, 8], BF16)
        onehot = sb1("onehot", [P, TOPK, TT, E], BF16)
        ends = sb1("ends", [P, E])
        base = sb1("base", [P, E])
        place = sb1("place", [P, TT, E])
        slotf = sb1("slotf", [P, TOPK, TT])
        owner = sb1("owner", [P, 1])
        ownerb = sb1("ownerb", [P, 1], BF16)
        early.close()

        got = sb("got", [P, 4, D])
        part = sb("part", [P, D])
        wqk_in = sb("wqk_in", [P, 2, 2 * HC * HD + 2])
        wv_in = sb("wv_in", [P, HC * 2 * HD])
        wo_in = sb("wo_in", [P, 2, D])
        wqk_r = sb("wqk_r", [P, 2, 2, 2 * HC * HD], F32R)
        wv_r = sb("wv_r", [P, 2, HC * 2 * HD], F32R)
        wo_r = sb("wo_r", [P, 2, 2, D], F32R)

        early = ExitStack()
        pair = sb1("pair", [P, 2, TT, E], BF16)
        placed = sb1("placed", [P, TT, E])
        chosen = sb1("chosen", [P, TT, E], BF16)
        ntile = sb1("ntile", [E, P])
        ntileb = sb1("ntileb", [E, P], BF16)
        gates_sb = sb1("gates_sb", [P, HC, E + 1])
        owners = sb1("owners", [1, P], I32)
        bo_sb = sb1("bo_sb", [P, D])
        sgate = sb1("sgate", [P, TT])
        wup_r = sb1("wup_r", [P, 2, SHARED, HC * 2 * I], F32R)
        wdn_r = sb1("wdn_r", [IH, 2, SHARED, 2 * D], F32R)
        x_t = sb1("x_t", [P, RING, D])
        wup = sb1("wup", [P, RING, HC * 2 * I])
        wdn = sb1("wdn", [IH, RING, 2 * D])
        xT_r = sb1("xT_r", [P, 2, 2, HC * P], F32R)
        sil = sb1("sil", [P, 2, I])
        hid = sb1("hid", [P, 2, I])
        hT_r = sb1("hT_r", [IH, 2, 2, 2 * P], F32R)
        assert RING + Y_RING >= NH and RING % SHARED == 0 and RING % Y_RING == 0
        early.close()

        qT_r = sb("qT_r", [P, 2, SEQ], F32R)
        kT_r = sb("kT_r", [P, 2, SEQ], F32R)
        v_r = sb("v_r", [P, 2, 2, QT, 2 * HD], F32R)
        prob = sb("prob", [P, PCOLS])
        probT_r = sb("probT_r", [P, 2, PT_COLS], F32R)
        oT_r = sb("oT_r", [P, 2, SEQ], F32R)

        def value(ap):
            return ap.bitcast(F32)

        ld_x = [sem(f"ld_x{k}") for k in range(2)]
        ld_gates, ld_bias = sem("ld_gates"), sem("ld_bias")
        ld_shared = [sem(f"ld_shared{k}") for k in range(SHARED)]
        zeroed, scattered, out_st = sem("zeroed"), sem("scattered"), sem("out_st")
        ld_up, ld_dn = ([sem(f"ld_{n}{k}") for k in range(RING)] for n in ("up", "dn"))
        ld_xt = [sem(f"ld_xt{k}") for k in range(RING // 2)]
        y_st = [sem(f"y_st{k}") for k in range(Y_RING // 2)]
        fetched = [sem(f"fetched{k}") for k in range(4)]
        ld_qk = [sem(f"ld_qk{k}") for k in range(2)]
        ld_o = [sem(f"ld_o{k}") for k in range(2)]
        ld_v, ld_wo_all = sem("ld_v"), [sem(f"ld_wo_all{k}") for k in range(2)]
        split_qk = [sem(f"split_qk{k}") for k in range(2)]
        split_o = [sem(f"split_o{k}") for k in range(2)]
        split_v, split_hi, bias_cp = sem("split_v"), sem("split_hi"), sem("bias_cp")
        split_sh, split_sh_hi = sem("split_sh"), [sem(f"split_sh_hi{k}") for k in range(SHARED)]
        const0, const1, const2 = sem("const0"), sem("const1"), sem("const2")
        dve_chain, xn_rdy = sem("dve_chain"), sem("xn_rdy")
        var_rdy, root_rdy = sem("var_rdy"), sem("root_rdy")
        bias_part_rdy, bias_ps, bias_rdy, bias_add = (
            sem("bias_" + n) for n in ("part_rdy", "ps", "rdy", "add"))
        xnT_ps, xnT_rdy, xnT_hi, xnT_lo = (sem("xnT_" + n) for n in ("ps", "rdy", "hi", "lo"))
        gate_ps, sg_exp = sem("gate_ps"), sem("sg_exp")
        rt_shift, rt_exp, rt_chosen, rt_ntile, rt_owner = (
            sem("rt_" + n) for n in ("shift", "exp", "chosen", "ntile", "owner"))
        count_ps, start_ps, owner_ps = sem("count_ps"), sem("start_ps"), sem("owner_ps")
        place_rdy = sem("place_rdy")
        slots_rdy, owners_rdy = sem("slots_rdy"), sem("owners_rdy")
        s_h, s_sil, s_hid, s_hTp, s_hTh, s_hT, s_y, s_acc = (
            sem("s_" + n) for n in ("h", "sil", "hid", "hTp", "hTh", "hT", "y", "acc"))
        e_xTp, e_xTh, e_xT, e_h, e_sil, e_hid, e_hTp, e_hTh, e_hT, e_y, e_yc, e_uph, e_up, e_dnh, e_dn = (
            sem("e_" + n) for n in ("xTp", "xTh", "xT", "h", "sil", "hid", "hTp", "hTh", "hT", "y", "yc",
                                    "uph", "up", "dnh", "dn"))
        scaled, summed = sem("scaled"), sem("summed")
        a_q, a_k, a_v, a_qh, a_kh, a_vh, a_qs, a_ks, a_vs = (
            sem("a_" + n) for n in ("q", "k", "v", "qh", "kh", "vh", "qs", "ks", "vs"))
        a_s, a_mx, a_max, a_exp, a_tp, a_pth, a_pt, a_pv, a_oth, a_ot = (
            sem("a_" + n) for n in ("s", "mx", "max", "exp", "tp", "pth", "pt", "pv", "oth", "ot"))
        a_rs, a_out, a_acc, pad_rdy = sem("a_rs"), sem("a_out"), sem("a_acc"), sem("pad_rdy")
        total = sem("total")

        block = ctx.enter_context(nc.Block())

        @block.sync
        def _(sp):
            tokens = x.rearrange("(t p) d -> p t d", p=P)
            for g in range(2):
                half = slice(g * TT // 2, (g + 1) * TT // 2)
                sp.dma_start(acc[:, half, :], tokens[:, half, :]).then_inc(ld_x[g], 16)
            sp.dma_start(gates_sb[:, :, :], gates).then_inc(ld_gates, 16)
            for q in range(SHARED):
                sp.dma_start(wup[:, q, :], w_up[E + q]).then_inc(ld_shared[q], 16)
                sp.dma_start(wdn[:, q, :], w_down[E + q]).then_inc(ld_shared[q], 16)
            sp.wait_ge(const0, 1)
            flat = x_slots.rearrange("(p r) d -> p (r d)", p=P)
            width = TILES * D // ZERO_PARTS
            for k in range(ZERO_PARTS):
                sp.dma_start(flat[:, k * width:(k + 1) * width], zeros[:, :]).then_inc(zeroed, 16)
            sp.dma_start(bvT[:, :], b_v).then_inc(ld_bias, 16)
            sp.dma_start(bo_sb[:, :], b_o.to_broadcast([P, D])).then_inc(ld_bias, 16)
            for g, (buffer, heads) in enumerate(((x_t[:, :, :], slice(0, RING)), (y_sb[:, 0:NH - RING, :], slice(RING, NH)))):
                sp.dma_start(buffer, w_o[heads].rearrange("h p n -> p h n")).then_inc(ld_wo_all[g], 16)
            def load_weights(i, k):
                e = sp.value_load(owners[0:1, bass.ds(i, 1)], min_val=0, max_val=E - 1)
                if due(i - RING + 1):
                    sp.wait_ge(e_up, i - RING + 1)
                sp.dma_start(wup[:, k, :], w_up[bass.ds(e, 1)].rearrange("s p n -> p (s n)")).then_inc(ld_up[k], 16)
                if due(i - RING + 1):
                    sp.wait_ge(e_dn, i - RING + 1)
                sp.dma_start(wdn[:, k, :], w_down[bass.ds(e, 1)].rearrange("s p n -> p (s n)")).then_inc(ld_dn[k], 16)

            sp.wait_ge(split_sh, SHARED)
            sp.wait_ge(owners_rdy, 1)
            for i in range(RING):
                load_weights(i, i)
            sp.wait_ge(bias_part_rdy, NH)
            sp.wait_ge(scattered, 16 * TOPK * TT)
            for k in range(0, RING, 2):
                sp.dma_start(x_t[:, k:k + 2, :], tile_rows(x_slots, k, 2)).then_inc(ld_xt[k // 2], 16)
            with sp.Fori(1, TILES // RING) as n:
                for k in range(RING):
                    load_weights(n * RING + k, k)
            for i in range(TILES // RING * RING, TILES):
                load_weights(i, i % RING)

            def load_pair(n):
                for h in range(2):
                    if due(n):
                        sp.wait_ge(split_qk[h], n)
                    sp.dma_start(wqk_in[:, h, :], w_qk[bass.ds(2 * n + h, 1)].rearrange("s p n -> p (s n)")).then_inc(ld_qk[h], 16)
                if due(n):
                    sp.wait_ge(split_v, n)
                sp.dma_start(wv_in[:, :], w_v[bass.ds(n, 1)].rearrange("s p n -> p (s n)")).then_inc(ld_v, 16)
                for h in range(2):
                    if due(n):
                        sp.wait_ge(split_o[h], n)
                    sp.dma_start(wo_in[:, h, :], w_o[bass.ds(2 * n + h, 1)].rearrange("s p n -> p (s n)")).then_inc(ld_o[h], 16)

            sp.wait_ge(bias_add, TT)
            load_pair(0)
            with sp.Fori(1, NH // 2) as n:
                load_pair(n)
            for t in range(TT):
                if t < QT:
                    sp.wait_ge(total, t + 1)
                else:
                    sp.wait_ge(a_acc, 2 * UNITS - 1 + (t - QT) // 2)
                sp.dma_start(out[t * P:(t + 1) * P, :], acc[:, t, :]).then_inc(out_st, 16)
            sp.wait_ge(out_st, 16 * TT)

        def combine(pool, n):
            t, j = divmod(n, TOPK)
            weight = top[:, t, j:j + 1]
            sums_before = (TOPK - 1) * t + max(j - 1, 0)
            pool.wait_ge(fetched[n % 4], 16 * (n // 4 + 1))
            if due(sums_before):
                pool.wait_ge(summed, sums_before)
            into = moe[:, t, :] if j == 0 else part[:, :]
            pool.tensor_scalar(into, got[:, n % 4, :], weight, None, ALU.mult).then_inc(scaled, 1)
            if j:
                pool.wait_ge(scaled, n + 1)
                pool.tensor_tensor(moe[:, t, :], moe[:, t, :], part[:, :], ALU.add).then_inc(summed, 1)

        @block.gpsimd
        def _(pool):
            pool.memset(zeros[:, :], 0.0).then_inc(const0, 1)
            pool.memset(ident[:, :], 0.0).then_inc(const1, 1)
            pool.memset(identb[:, :], 0.0).then_inc(const1, 1)
            pool.memset(maskb[:, :], 0.0).then_inc(const1, 1)
            pool.memset(earlier[:, :], 1.0).then_inc(const1, 1)
            pool.memset(upto[:, :], 1.0).then_inc(const1, 1)
            pool.memset(onesb[:, :], 1.0).then_inc(const1, 1)
            pool.memset(ones[:, :], 1.0).then_inc(const1, 1)
            pool.wait_ge(const1, 7)
            for m in (ident, identb):
                pool.affine_select(out=m[:, :], in_=m[:, :], compare_op=ALU.not_equal, fill=1.0,
                                   base=0, pattern=[[-1, P]], channel_multiplier=1).then_inc(const2, 1)
            pool.affine_select(out=maskb[:, :], in_=maskb[:, :], compare_op=ALU.is_ge, fill=MASKED / SCALE,
                               base=0, pattern=[[-1, P]], channel_multiplier=1).then_inc(const2, 1)
            pool.affine_select(out=earlier[:, :], in_=earlier[:, :], compare_op=ALU.is_ge, fill=0.0,
                               base=-1, pattern=[[1, P]], channel_multiplier=-1).then_inc(const2, 1)
            pool.affine_select(out=upto[:, :], in_=upto[:, :], compare_op=ALU.is_ge, fill=0.0,
                               base=0, pattern=[[1, P]], channel_multiplier=-1).then_inc(const2, 1)
            pool.iota(iota_e[:, :], pattern=[[1, E]], base=0, channel_multiplier=0, allow_small_or_imprecise_dtypes=True).then_inc(const2, 1)
            pool.iota(iota_p[:, :], pattern=[[1, 1]], base=0, channel_multiplier=1, allow_small_or_imprecise_dtypes=True).then_inc(const2, 1)
            for q in range(SHARED):
                pool.wait_ge(split_sh_hi[q], 2)
                pool.tensor_tensor(wup_r[:, LO, q, :], wup[:, q, :], value(wup_r[:, HI, q, :]), ALU.subtract)
                pool.tensor_tensor(wdn_r[:, LO, q, :], wdn[:, q, :], value(wdn_r[:, HI, q, :]), ALU.subtract).then_inc(split_sh, 1)

            def scatter(j):
                pool.wait_ge(slots_rdy, j + 1)
                for t in range(TT):
                    pool.indirect_dma_start(
                        out=x_slots[:, :], out_offset=bass.IndirectOffsetOnAxis(ap=slot[:, j, t:t + 1], axis=0),
                        in_=xn[:, t, :], in_offset=None).then_inc(scattered, 16)

            pool.wait_ge(zeroed, 16 * ZERO_PARTS)
            for j in range(TOPK):
                scatter(j)

            def e_step(i, j, r):
                if exists(i + 4, TILES):
                    w = (j + 4) % SHARED
                    pool.wait_ge(e_uph, i + 5)
                    pool.tensor_tensor(wup_r[:, LO, w, :], wup[:, (j + 4) % RING, :], value(wup_r[:, HI, w, :]),
                                       ALU.subtract).then_inc(e_up, 1)

            run_tiles(pool, e_step)

            def split(source, hi, lo, n, done):
                if n >= 5:
                    pool.tensor_copy(hi, source).then_inc(split_hi, 1)
                pool.wait_ge(split_hi, n + 1)
                pool.tensor_tensor(lo, source, value(hi), ALU.subtract).then_inc(done, 1)

            for n in range(NH // 2):
                for h in range(2):
                    pool.wait_ge(ld_qk[h], 16 * n + 16)
                    if due(n):
                        pool.wait_ge(a_k, 4 * n - 1 + h)
                        pool.wait_ge(a_qs, 4 * n - 1 + h)
                        pool.wait_ge(a_ks, 4 * n - 1 + h)
                    pool.tensor_copy(bias_qk[:, h, :], wqk_in[:, h, 4 * HD:4 * HD + 2]).then_inc(bias_cp, 1)
                    split(wqk_in[:, h, 0:4 * HD], wqk_r[:, h, HI, :], wqk_r[:, h, LO, :], 5 * n + 2 * h, split_qk[h])
                    if h == 0:
                        pool.wait_ge(ld_v, 16 * n + 16)
                        if due(n):
                            pool.wait_ge(a_v, 4 * n)
                        split(wv_in[:, :], wv_r[:, HI, :], wv_r[:, LO, :], 5 * n + 1, split_v)
                for h in range(2):
                    pool.wait_ge(ld_o[h], 16 * n + 16)
                    if due(n):
                        pool.wait_ge(a_out, 2 * (4 * n - 1 + h))
                    split(wo_in[:, h, :], wo_r[:, h, HI, :], wo_r[:, h, LO, :], 5 * n + 3 + h, split_o[h])
                if n == 0:
                    for k in range(Y_RING // 2):
                        pool.wait_ge(y_st[k], 16 * ((TILES - 1 - 2 * k) // Y_RING + 1))
                for j in range(TOPK):
                    if due(n):
                        pool.wait_ge(scaled, TOPK * (n - 1) + j + 1)
                    pool.indirect_dma_start(
                        out=got[:, j, :], out_offset=None, in_=y_slots[:, :],
                        in_offset=bass.IndirectOffsetOnAxis(ap=slot[:, j, n:n + 1], axis=0)).then_inc(fetched[j], 16)
                for j in range(TOPK):
                    combine(pool, TOPK * n + j)

        @block.tensor
        def _(pe):
            def three(out_, stationary, moving, first=True, last=True):
                for m, (a, b) in enumerate(PASSES):
                    ins = pe.matmul(out_, stationary(a), moving(b), start=first and m == 0, stop=last and m == 2)
                return ins

            pe.wait_ge(const2, 7)
            for _ in range(WARM_UP):
                pe.matmul(banks[7][:, :], identb[:, :], identb[:, None, :].to_broadcast([P, 4, P]), start=True, stop=True)
            for n in range(2 * HC):
                c, g = n % HC, n // HC
                for m in range(4):
                    t = 4 * g + m
                    pe.wait_ge(xn_rdy, t + 1)
                    ins = pe.transpose(banks[n][:, m * P:(m + 1) * P], xn[:, t, c * P:(c + 1) * P], ident[:, :])
                ins.then_inc(xnT_ps, 1)
            pe.wait_ge(ld_gates, 16)
            for t in range(TT):
                if t % 4 == 0:
                    pe.wait_ge(xnT_rdy, HC * (t // 4 + 1))
                for c in range(HC):
                    ins = pe.matmul(banks[4][:, t * 64:t * 64 + E + 1], xnT[:, c, t * P:(t + 1) * P],
                                    gates_sb[:, c, :], start=c == 0, stop=c == HC - 1)
            ins.then_inc(gate_ps, 1)

            def ranks():
                pe.wait_ge(rt_chosen, 1)
                pe.wait_ge(sg_exp, 1)
                for t in range(TT):
                    for s in range(t + 1):
                        pe.matmul(banks[5][:, t * E:(t + 1) * E], (earlier if s == t else onesb)[:, :],
                                  chosen[:, s, :], start=s == 0, stop=s == t)
                for t in range(TT):
                    ins = pe.matmul(banks[4][0:E, 0:P], chosen[:, t, :], onesb[:, :], start=t == 0, stop=t == TT - 1)
                ins.then_inc(count_ps, 1)

            def starts():
                pe.wait_ge(rt_ntile, 1)
                pe.matmul(banks[4][:, 0:E], ntileb[:, :], earlier[0:E, 0:E], start=True, stop=True)
                pe.matmul(banks[4][:, 64:64 + E], ntileb[:, :], upto[0:E, 0:E], start=True, stop=True).then_inc(start_ps, 1)

            def owner_row():
                pe.wait_ge(rt_owner, 1)
                pe.matmul(banks[4][0:1, 0:P], ownerb[:, :], identb[:, :], start=True, stop=True).then_inc(owner_ps, 1)

            def bias_row():
                pe.wait_ge(bias_part_rdy, NH)
                pe.wait_ge(place_rdy, 1)
                pe.matmul(banks[5][:, 0:D], ones[:, :].to_broadcast([P, P]), bias_part[:, :],
                          start=True, stop=True).then_inc(bias_ps, 1)

            last = SHARED * TT - 1
            along = {7: ranks, 9: starts, 11: owner_row, BIAS_STEP: bias_row}

            def s_step(k):
                if k in along:
                    along[k]()
                if exists(k + 1, last + 1):
                    t1, q1 = divmod(k + 1, SHARED)
                    if t1 == 0:
                        pe.wait_ge(split_sh, q1 + 1)
                    if due(k):
                        pe.wait_ge(s_sil, k)
                        pe.wait_ge(s_hid, k)
                    for c in range(HC):
                        ins = three(banks[q1 % 2][:, 0:2 * I], lambda a: xnT_r[:, a, c, t1 * P:(t1 + 1) * P],
                                    lambda a: wup_r[:, a, q1, c * 2 * I:(c + 1) * 2 * I], c == 0, c == HC - 1)
                    ins.then_inc(s_h, 1)
                if exists(k, last + 1):
                    pe.wait_ge(s_hid, k + 1)
                    if due(k - 1):
                        pe.wait_ge(s_hT, k - 1)
                    for c in range(2):
                        ins = pe.transpose(banks[2 + k % 2][0:IH, c * P:(c + 1) * P],
                                           hid[:, k % 2, c * IH:(c + 1) * IH], ident[:, :])
                    ins.then_inc(s_hTp, 1)
                if exists(k - 1, last + 1):
                    t0, q0 = divmod(k - 1, SHARED)
                    pe.wait_ge(s_hT, k)
                    if q0 == 0 and due(t0 - 1):
                        pe.wait_ge(s_acc, t0 - 1)
                    for c in range(2):
                        ins = three(banks[6 + t0 % 2][:, 0:D], lambda a: hT_r[:, (k - 1) % 2, a, c * P:(c + 1) * P],
                                    lambda a: wdn_r[:, a, q0, c * D:(c + 1) * D],
                                    q0 == 0 and c == 0, q0 == SHARED - 1 and c == 1)
                    ins.then_inc(s_y, 1)

            pe.wait_ge(xnT_lo, 4)
            run_shared(s_step)

            pe.wait_ge(s_acc, TT)
            pe.wait_ge(owners_rdy, 1)
            pe.wait_ge(bias_rdy, 1)

            def e_step(i, j, r):
                if exists(i + 1, TILES):
                    w, b = (j + 1) % SHARED, (j + 1) % 2
                    pe.wait_ge(e_xT, i + 2)
                    pe.wait_ge(e_up, i + 2)
                    if due(i):
                        pe.wait_ge(e_sil, i)
                        pe.wait_ge(e_hid, i)
                    for c in range(HC):
                        ins = three(banks[b][:, 0:2 * I], lambda a: xT_r[:, b, a, c * P:(c + 1) * P],
                                    lambda a: wup_r[:, a, w, c * 2 * I:(c + 1) * 2 * I], c == 0, c == HC - 1)
                    ins.then_inc(e_h, 1)
                if exists(i, TILES):
                    pe.wait_ge(e_hid, i + 1)
                    if due(i - 1):
                        pe.wait_ge(e_hT, i - 1)
                    for c in range(2):
                        ins = pe.transpose(banks[2 + j % 2][0:IH, c * P:(c + 1) * P],
                                           hid[:, j % 2, c * IH:(c + 1) * IH], ident[:, :])
                    ins.then_inc(e_hTp, 1)
                if exists(i + 3, TILES):
                    k, b = (j + 3) % RING, (j + 3) % 2
                    pe.wait_ge(ld_xt[k // 2], 16 * (round_of(j, r, 3, RING) + 1))
                    if due(i + 2):
                        pe.wait_ge(e_xT, i + 2)
                    for c in range(HC):
                        ins = pe.transpose(banks[4 + b][:, c * P:(c + 1) * P], x_t[:, k, c * P:(c + 1) * P], ident[:, :])
                    ins.then_inc(e_xTp, 1)
                if exists(i - 1, TILES):
                    w, b = (j - 1) % SHARED, (j - 1) % 2
                    pe.wait_ge(e_hT, i)
                    pe.wait_ge(e_dn, i)
                    if due(i - 2):
                        pe.wait_ge(e_yc, i - 2)
                    for c in range(2):
                        ins = three(banks[6 + b][:, 0:D], lambda a: hT_r[:, b, a, c * P:(c + 1) * P],
                                    lambda a: wdn_r[:, a, w, c * D:(c + 1) * D], c == 0, c == 1)
                    ins.then_inc(e_y, 1)

            run_tiles(pe, e_step)

            pe.wait_ge(e_yc, TILES)

            def project(u, j, n):
                h, b = j % 2, j // 2
                pe.wait_ge(split_qk[h], n + 1)
                for which, done in ((0, a_q), (1, a_k)):
                    if h == 1:
                        pe.wait_ge(a_vs, u + which)
                    elif isinstance(u, int) and u == 2:
                        pe.wait_ge((a_qs, a_ks)[which], 2)
                    elif due(u):
                        pe.wait_ge(a_acc, 2 * (u - 3) + 1 + which)
                    for c in range(HC):
                        at = (which * HC + c) * HD
                        ins = three(banks[6 + which][:, :], lambda a: wqk_r[:, h, a, at:at + HD],
                                    lambda a: xnT_r[:, a, c, b * SEQ:(b + 1) * SEQ], c == 0, c == HC - 1)
                    ins.then_inc(done, 1)

            def project_values(u, j, n):
                b = j // 2
                pe.wait_ge(split_v, n + 1)
                for g in range(2):
                    if due(u - 1):
                        pe.wait_ge(a_acc, 2 * (u - 2) + 1 + g)
                    else:
                        pe.wait_ge((a_qs, a_ks)[g], u + 1)
                    for m in range(2):
                        t = b * QT + 2 * g + m
                        for c in range(HC):
                            ins = three(banks[6 + g][:, m * 2 * HD:(m + 1) * 2 * HD],
                                        lambda a: xnT_r[:, a, c, t * P:(t + 1) * P],
                                        lambda a: wv_r[:, a, c * 2 * HD:(c + 1) * 2 * HD], c == 0, c == HC - 1)
                    ins.then_inc(a_v, 1)

            def scores(u):
                pe.wait_ge(a_qs, u + 1)
                pe.wait_ge(a_ks, u + 1)
                if due(u):
                    pe.wait_ge(a_exp, 3 * u)
                    pe.wait_ge(a_pt, 3 * u - 2)
                for q, bank, at, keys in SCORES:
                    three(banks[bank][:, at:at + keys], lambda a: qT_r[:, a, q * P:(q + 1) * P],
                          lambda a: kT_r[:, a, 0:keys], first=q != 1, last=False)
                    blocks = (0, 2, 1, 1)[q]
                    if blocks:
                        pe.matmul(banks[bank][:, at + q * P:at + (q + blocks) * P], identb[:, :],
                                  maskb[:, None, :].to_broadcast([P, blocks, P]), start=False, stop=True).then_inc(a_s, 1)

            def transposes(u):
                pe.wait_ge(a_exp, 3 * u + 3)
                if due(u):
                    pe.wait_ge(a_pt, 3 * u)
                for bank, keys in ((1, (2,)), (3, (0,)), (4, (3, 1))):
                    at = 0
                    for k in keys:
                        for q in range(k, QT):
                            ins = pe.transpose(banks[bank][:, at:at + P],
                                               prob[:, P_AT[q] + k * P:P_AT[q] + (k + 1) * P], ident[:, :])
                            at += P
                    ins.then_inc(a_tp, 1)

            def output(u, j, n):
                h = j % 2
                pe.wait_ge(a_ot, u + 1)
                pe.wait_ge(split_o[h], n + 1)
                for g in range(2):
                    if isinstance(u, int) and u + 2 >= UNITS:
                        pe.wait_ge(a_acc, 2 * u - 1 + g)
                    else:
                        pe.wait_ge((a_qs, a_ks)[g], u + 3)
                    for m in range(2):
                        q = 2 * g + m
                        ins = three(banks[6 + g][:, m * D:(m + 1) * D], lambda a: oT_r[:, a, q * P:(q + 1) * P],
                                    lambda a: wo_r[:, h, a, :])
                    ins.then_inc(a_out, 1)

            def weigh(u, j):
                h, b = j % 2, j // 2
                pe.wait_ge(a_pt, 3 * u + 3)
                pe.wait_ge(a_vs, u + 2 - h)
                if due(u):
                    pe.wait_ge(a_ot, u)
                else:
                    pe.wait_ge(pad_rdy, 1)
                for k in range(QT):
                    cols = SEQ - PT_FROM[k]
                    ins = three(banks[5][:, PT_FROM[k]:SEQ], lambda a: v_r[:, a, b, k, h * HD:(h + 1) * HD],
                                lambda a: probT_r[:, a, PT_AT[k]:PT_AT[k] + cols], k == 0, k == QT - 1)
                ins.then_inc(a_pv, 1)

            def a_step(u, j, n):
                if exists(u + 1, UNITS):
                    project(u + 1, (j + 1) % 4, n + (j == 3))
                if exists(u, UNITS):
                    transposes(u)
                if exists(u - 1, UNITS):
                    output(u - 1, (j - 1) % 4, n - (j == 0))
                if exists(u + 1, UNITS):
                    scores(u + 1)
                    if (j + 1) % 2 == 0:
                        project_values(u + 1, (j + 1) % 4, n + (j == 3))
                if exists(u, UNITS):
                    weigh(u, j)

            run_units(pe, a_step)

        @block.scalar
        def _(act):
            act.wait_ge(var_rdy, 1)
            act.activation(root[:, :], vareps[:, :], ACT.Sqrt).then_inc(root_rdy, 1)
            for n in range(2 * HC):
                c, g = n % HC, n // HC
                act.wait_ge(xnT_ps, n + 1)
                cols = slice(g * 4 * P, (g + 1) * 4 * P)
                act.activation(xnT[:, c, cols], banks[n][:, :], ACT.Copy).then_inc(xnT_rdy, 1)
            for n in range(2 * HC):
                c, g = n % HC, n // HC
                act.activation(xnT_r[:, HI, c, g * 4 * P:(g + 1) * 4 * P], banks[n][:, :], ACT.Copy).then_inc(xnT_hi, 1)
            for q in range(2, SHARED):
                act.wait_ge(ld_shared[q], 32)
                act.activation(wup_r[:, HI, q, :], wup[:, q, :], ACT.Copy).then_inc(split_sh_hi[q], 1)
                act.activation(wdn_r[:, HI, q, :], wdn[:, q, :], ACT.Copy).then_inc(split_sh_hi[q], 1)
            act.wait_ge(rt_shift, 1)
            act.activation(probs[:, :, :], shifted[:, :, :], ACT.Exp).then_inc(rt_exp, 1)
            logits = banks[4][:, :].rearrange("p (t e) -> p t e", e=64)
            act.activation(sgate[:, :], logits[:, :, E:E + 1].rearrange("p t a -> p (t a)"), ACT.Exp,
                           scale=-1.0).then_inc(sg_exp, 1)

            def s_step(k):
                if exists(k + 1, SHARED * TT):
                    b = (k + 1) % 2
                    act.wait_ge(s_h, k + 2)
                    if due(k):
                        act.wait_ge(s_hid, k)
                    act.activation(sil[:, b, :], banks[b][:, 0:I], ACT.Silu).then_inc(s_sil, 1)
                if exists(k, SHARED * TT):
                    b = k % 2
                    act.wait_ge(s_hTp, k + 1)
                    if due(k - 1):
                        act.wait_ge(s_y, k - 1)
                    act.activation(hT_r[:, b, HI, :], banks[2 + b][0:IH, 0:2 * P], ACT.Copy).then_inc(s_hTh, 1)
                if exists(k - (SHARED * TT - EARLY), EARLY):
                    m = k - (SHARED * TT - EARLY)
                    act.wait_ge(ld_up[m], 16)
                    act.wait_ge(s_h, SHARED * (TT - 1) + m + 1)
                    act.activation(wup_r[:, HI, m, :], wup[:, m, :], ACT.Copy).then_inc(e_uph, 1)

            run_shared(s_step)

            def e_step(i, j, r):
                if exists(i + 1, TILES):
                    b = (j + 1) % 2
                    act.wait_ge(e_h, i + 2)
                    if due(i):
                        act.wait_ge(e_hid, i)
                    act.activation(sil[:, b, :], banks[b][:, 0:I], ACT.Silu).then_inc(e_sil, 1)
                if exists(i, TILES):
                    b = j % 2
                    act.wait_ge(e_hTp, i + 1)
                    if due(i - 1):
                        act.wait_ge(e_y, i - 1)
                    act.activation(hT_r[:, b, HI, :], banks[2 + b][0:IH, 0:2 * P], ACT.Copy).then_inc(e_hTh, 1)
                if exists(i + 3, TILES):
                    b = (j + 3) % 2
                    act.wait_ge(e_xTp, i + 4)
                    if due(i + 2):
                        act.wait_ge(e_h, i + 2)
                    act.activation(xT_r[:, b, HI, :], banks[4 + b][:, 0:HC * P], ACT.Copy).then_inc(e_xTh, 1)
                if (j + 3) % 2 and exists(i + 2, TILES - RING):
                    k, count = (j + 2) % RING, tiles_left(i + 2 + RING)
                    act.dma_start(x_t[:, k:k + count, :], tile_rows(x_slots, i + 2 + RING, count)).then_inc(ld_xt[k // 2], 16)
                if exists(i + 4 - EARLY, TILES - EARLY):
                    k, w = (j + 4) % RING, (j + 4) % SHARED
                    act.wait_ge(ld_up[k], 16 * (round_of(j, r, 4, RING) + 1))
                    if due(i + 1):
                        act.wait_ge(e_h, i + 1)
                    act.activation(wup_r[:, HI, w, :], wup[:, k, :], ACT.Copy).then_inc(e_uph, 1)
                if exists(i - 1, TILES):
                    b, k = (j - 1) % 2, (j - 1) % Y_RING
                    act.wait_ge(e_y, i)
                    before = round_of(j, r, -1, Y_RING)
                    if due(before):
                        act.wait_ge(y_st[k // 2], 16 * before)
                    act.activation(y_sb[:, k, :], banks[6 + b][:, 0:D], ACT.Copy).then_inc(e_yc, 1)
                if isinstance(i, int) and i >= TILES - 4:
                    first_pair_hi(i - (TILES - 4))
                if j % 2 and exists(i - 3, TILES):
                    k, count = (j - 3) % Y_RING, tiles_left(i - 3)
                    act.wait_ge(e_yc, i - 3 + count)
                    act.dma_start(tile_rows(y_slots, i - 3, count), y_sb[:, k:k + count, :]).then_inc(y_st[k // 2], 16)

            def first_pair_hi(part):
                def qk(h):
                    act.wait_ge(ld_qk[h], 16)
                    act.activation(wqk_r[:, h, HI, :], wqk_in[:, h, 0:4 * HD], ACT.Copy).then_inc(split_hi, 1)

                if part == 0:
                    qk(0)
                if part == 1:
                    act.wait_ge(ld_v, 16)
                    act.activation(wv_r[:, HI, :], wv_in[:, :], ACT.Copy).then_inc(split_hi, 1)
                if part == 2:
                    qk(1)
                if part == 3:
                    for h in range(2):
                        act.wait_ge(ld_o[h], 16)
                        act.activation(wo_r[:, h, HI, :], wo_in[:, h, :], ACT.Copy).then_inc(split_hi, 1)

            act.wait_ge(s_y, SHARED * TT)
            run_tiles(act, e_step)

            def values_hi(u, j, g):
                act.wait_ge(a_v, u + 1 + g)
                if due(u - 2):
                    act.wait_ge(a_pv, u - 2)
                act.activation(v_r[:, HI, j // 2, 2 * g:2 * g + 2, :].rearrange("p t n -> p (t n)"),
                               banks[6 + g][:, :], ACT.Copy).then_inc(a_vh, 1)

            def a_step(u, j, n):
                if exists(u + 1, UNITS):
                    h, b = (j + 1) % 2, ((j + 1) % 4) // 2
                    if due(u + 1):
                        act.wait_ge(a_s, 3 * (u + 1))
                    act.wait_ge(a_q, u + 2)
                    act.activation(qT_r[:, HI, :], banks[6][:, :], ACT.Identity, bias=bias_qk[:, h, 0:1]).then_inc(a_qh, 1)
                    act.wait_ge(a_k, u + 2)
                    act.activation(kT_r[:, HI, :], banks[7][:, :], ACT.Identity, bias=bias_qk[:, h, 1:2]).then_inc(a_kh, 1)
                if exists(u, UNITS):
                    if due(u):
                        act.wait_ge(a_pv, u)
                    for m, (bank, at, to, cols) in enumerate(TRANSPOSED):
                        act.wait_ge(a_tp, 3 * u + 1 + m)
                        act.activation(probT_r[:, HI, to:to + cols], banks[bank][:, at:at + cols], ACT.Copy).then_inc(a_pth, 1)
                if exists(u + 1, UNITS):
                    b = (j + 1) % 2
                    alone = isinstance(u, int) and u < 0
                    if b == 0:
                        values_hi(u + 1, (j + 1) % 4, 0)
                    if b == 0 and alone:
                        values_hi(u + 1, (j + 1) % 4, 1)
                    if due(u + 1):
                        act.wait_ge(a_tp, 3 * (u + 1))
                    act.wait_ge(a_max, u + 2)
                    for q, bank, at, _ in SCORES:
                        keys = (q + 1) * P
                        ins = act.activation(prob[:, P_AT[q]:P_AT[q] + keys], banks[bank][:, at:at + keys], ACT.Exp,
                                             bias=nmaxs[:, b, q:q + 1], scale=SCALE, accum_out=sums[:, b, q:q + 1])
                        if q:
                            ins.then_inc(a_exp, 1)
                    if b == 0 and not alone:
                        values_hi(u + 1, (j + 1) % 4, 1)

            run_units(act, a_step)

        @block.vector
        def _(dve):
            chain = [0]

            def link(ins):
                chain[0] += 1
                ins.then_inc(dve_chain, 1)
                dve.wait_ge(dve_chain, chain[0])

            for t in range(TT):
                if t % (TT // 2) == 0:
                    dve.wait_ge(ld_x[t // (TT // 2)], 16)
                ins = dve.bn_stats(stats[:, t, :], acc[:, t, :])
            link(ins)
            for t in range(TT):
                ins = dve.bn_aggr(mv[:, t, :], stats[:, t, :])
            link(ins)
            dve.tensor_scalar(vareps[:, :], mv[:, :, 1], EPS, None, ALU.add).then_inc(var_rdy, 1)
            dve.wait_ge(root_rdy, 1)
            link(dve.reciprocal(rstd[:, :], root[:, :]))
            link(dve.tensor_tensor(root[:, :], rstd[:, :], rstd[:, :], ALU.mult))
            link(dve.tensor_tensor(root[:, :], root[:, :], vareps[:, :], ALU.mult))
            link(dve.tensor_scalar(root[:, :], root[:, :], -0.5, 1.5, ALU.mult, ALU.add))
            link(dve.tensor_tensor(rstd[:, :], rstd[:, :], root[:, :], ALU.mult))
            for t in range(TT):
                dve.tensor_scalar(xn[:, t, :], acc[:, t, :], mv[:, t, 0:1], rstd[:, t:t + 1],
                                  ALU.subtract, ALU.mult).then_inc(xn_rdy, 1)
            for q in range(2):
                dve.wait_ge(ld_shared[q], 32)
                dve.tensor_copy(wup_r[:, HI, q, :], wup[:, q, :]).then_inc(split_sh_hi[q], 1)
                dve.tensor_copy(wdn_r[:, HI, q, :], wdn[:, q, :]).then_inc(split_sh_hi[q], 1)
            for n in range(2 * HC):
                c, g = n % HC, n // HC
                cols = slice(g * 4 * P, (g + 1) * 4 * P)
                dve.wait_ge(xnT_hi, n + 1)
                dve.tensor_tensor(xnT_r[:, LO, c, cols], banks[n][:, :], value(xnT_r[:, HI, c, cols]),
                                  ALU.subtract).then_inc(xnT_lo, 1)

            logits = banks[4][:, :].rearrange("p (t e) -> p t e", e=64)[:, :, 0:E]
            over = [P, TT, E]
            dve.wait_ge(gate_ps, 1)
            dve.wait_ge(const2, 7)
            link(dve.tensor_reduce(lmax[:, :], logits, AX.X, ALU.max))
            dve.tensor_tensor(shifted[:, :, :], logits, lmax[:, :, None].to_broadcast(over), ALU.subtract).then_inc(rt_shift, 1)
            dve.wait_ge(sg_exp, 1)
            link(dve.tensor_scalar(sgate[:, :], sgate[:, :], 1.0, None, ALU.add))
            link(dve.reciprocal(sgate[:, :], sgate[:, :]))

            def exp_sums():
                dve.wait_ge(rt_exp, 1)
                link(dve.tensor_reduce(psum_e[:, :], probs[:, :, :], AX.X, ALU.add))
                link(dve.reciprocal(psum_e[:, :], psum_e[:, :]))

            def softmax():
                link(dve.tensor_tensor(probs[:, :, :], probs[:, :, :], psum_e[:, :, None].to_broadcast(over), ALU.mult))

            def largest():
                for t in range(TT):
                    ins = dve.max(top[:, t, :], probs[:, t, :])
                link(ins)

            def indices():
                for t in range(TT):
                    ins = dve.max_index(topi[:, t, :], top[:, t, :], probs[:, t, :])
                link(ins)
                link(dve.tensor_copy(topb[:, :, :], topi[:, :, :]))

            def onehots(choices_):
                for j in choices_:
                    ins = dve.tensor_tensor(onehot[:, j], iota_e[:, None, :].to_broadcast(over),
                                            topb[:, :, j:j + 1].to_broadcast(over), ALU.is_equal)
                link(ins)

            def choices():
                for j in range(2):
                    ins = dve.tensor_tensor(pair[:, j], onehot[:, 2 * j], onehot[:, 2 * j + 1], ALU.add)
                link(ins)
                dve.tensor_tensor(chosen[:, :, :], pair[:, 0], pair[:, 1], ALU.add).then_inc(rt_chosen, 1)

            def tile_counts():
                dve.wait_ge(count_ps, 1)
                link(dve.tensor_scalar(ntile[:, :], banks[4][0:E, 0:P], float(P - 1), 1.0 / P, ALU.add, ALU.mult))
                link(dve.tensor_scalar(ntile[:, :], ntile[:, :], -(P - 1) / (2.0 * P), ROUND, ALU.add, ALU.add))
                dve.tensor_scalar(ntileb[:, :], ntile[:, :], ROUND, None, ALU.subtract).then_inc(rt_ntile, 1)

            def tile_owners():
                dve.wait_ge(start_ps, 1)
                dve.tensor_scalar(base[:, :], banks[4][:, 0:E], float(P), None, ALU.mult)
                link(dve.tensor_scalar(ends[:, :], banks[4][:, 64:64 + E], iota_p[:, 0:1], None, ALU.is_le))
                link(dve.tensor_reduce(owner[:, :], ends[:, :], AX.X, ALU.add))
                dve.tensor_scalar(ownerb[:, :], owner[:, :], float(E - 1), None, ALU.min).then_inc(rt_owner, 1)
                dve.tensor_tensor(place[:, :, :], banks[5][:, 0:TT * E].rearrange("p (t e) -> p t e", e=E),
                                  base[:, None, :].to_broadcast(over), ALU.add).then_inc(place_rdy, 1)
                dve.wait_ge(place_rdy, 1)

            def owner_numbers():
                dve.wait_ge(owner_ps, 1)
                dve.tensor_copy(owners[:, :], banks[4][0:1, 0:P]).then_inc(owners_rdy, 1)

            def slots_of(choice):
                link(dve.tensor_tensor(placed[:, :, :], onehot[:, choice], place[:, :, :], ALU.mult))
                link(dve.tensor_reduce(slotf[:, choice, :], placed[:, :, :], AX.X, ALU.add))
                dve.tensor_copy(slot[:, choice, :], slotf[:, choice, :]).then_inc(slots_rdy, 1)

            def bias_heads(heads):
                for h in heads:
                    g, k = divmod(h, RING)
                    rows = (x_t, y_sb)[g][:, k, :]
                    if h == 0:
                        dve.wait_ge(ld_bias, 32)
                        dve.wait_ge(ld_wo_all[0], 16)
                        dve.wait_ge(ld_wo_all[1], 16)
                        dve.tensor_scalar(bias_part[:, :], rows, bvT[:, 0:1], None, ALU.mult).then_inc(bias_part_rdy, 1)
                    else:
                        dve.wait_ge(bias_part_rdy, h)
                        dve.scalar_tensor_tensor(out=bias_part[:, :], in0=rows, scalar=bvT[:, h:h + 1],
                                                 in1=bias_part[:, :], op0=ALU.mult, op1=ALU.add).then_inc(bias_part_rdy, 1)

            def bias_sum():
                dve.wait_ge(bias_ps, 1)
                dve.tensor_tensor(bo_sb[:, :], bo_sb[:, :], banks[5][:, 0:D], ALU.add).then_inc(bias_rdy, 1)

            def add_bias(t):
                dve.wait_ge(bias_rdy, 1)
                dve.wait_ge(s_acc, t + 1)
                dve.tensor_tensor(acc[:, t, :], acc[:, t, :], bo_sb[:, :], ALU.add).then_inc(bias_add, 1)

            along = {
                -1: exp_sums, 0: softmax, 1: largest, 2: indices, 3: lambda: onehots((0, 1)), 4: lambda: onehots((2, 3)),
                5: choices, 7: tile_counts, 9: tile_owners, 10: lambda: slots_of(0), 11: owner_numbers,
                12: lambda: slots_of(1), 14: lambda: slots_of(2), 16: lambda: slots_of(3), BIAS_STEP: bias_sum,
            }
            bias_steps = [k for k in range(13, BIAS_STEP - 1) if k not in along]
            assert len(bias_steps) >= NH // 2 and BIAS_STEP == SHARED * TT - TT + 1

            def s_step(k):
                if exists(k + 1, SHARED * TT):
                    b = (k + 1) % 2
                    dve.wait_ge(s_sil, k + 2)
                    if due(k):
                        dve.wait_ge(s_hTp, k)
                    dve.tensor_tensor(hid[:, b, :], sil[:, b, :], banks[b][:, I:2 * I], ALU.mult).then_inc(s_hid, 1)
                if exists(k, SHARED * TT):
                    b = k % 2
                    dve.wait_ge(s_hTh, k + 1)
                    dve.tensor_tensor(hT_r[:, b, LO, :], banks[2 + b][0:IH, 0:2 * P], value(hT_r[:, b, HI, :]),
                                      ALU.subtract).then_inc(s_hT, 1)
                if k > 0 and k % SHARED == 0:
                    t0 = k // SHARED - 1
                    dve.wait_ge(s_y, k)
                    dve.scalar_tensor_tensor(out=acc[:, t0, :], in0=banks[6 + t0 % 2][:, 0:D], scalar=sgate[:, t0:t0 + 1],
                                             in1=acc[:, t0, :], op0=ALU.mult, op1=ALU.add).then_inc(s_acc, 1)
                if k in along:
                    along[k]()
                if k in bias_steps[-(NH // 2):]:
                    at = 2 * bias_steps[-(NH // 2):].index(k)
                    bias_heads((at, at + 1))
                if k > SHARED * TT - TT:
                    add_bias(k - (SHARED * TT - TT) - 1)

            run_shared(s_step)

            def e_step(i, j, r):
                if exists(i + 1, TILES):
                    b = (j + 1) % 2
                    dve.wait_ge(e_sil, i + 2)
                    if due(i):
                        dve.wait_ge(e_hTp, i)
                    dve.tensor_tensor(hid[:, b, :], sil[:, b, :], banks[b][:, I:2 * I], ALU.mult).then_inc(e_hid, 1)
                if exists(i, TILES):
                    b = j % 2
                    dve.wait_ge(e_hTh, i + 1)
                    dve.tensor_tensor(hT_r[:, b, LO, :], banks[2 + b][0:IH, 0:2 * P], value(hT_r[:, b, HI, :]),
                                      ALU.subtract).then_inc(e_hT, 1)
                if exists(i + 3, TILES):
                    b = (j + 3) % 2
                    dve.wait_ge(e_xTh, i + 4)
                    dve.tensor_tensor(xT_r[:, b, LO, :], banks[4 + b][:, 0:HC * P], value(xT_r[:, b, HI, :]),
                                      ALU.subtract).then_inc(e_xT, 1)
                if exists(i + 2, TILES):
                    k, w = (j + 2) % RING, (j + 2) % SHARED
                    dve.wait_ge(ld_dn[k], 16 * (round_of(j, r, 2, RING) + 1))
                    if due(i - 1):
                        dve.wait_ge(e_y, i - 1)
                    dve.tensor_copy(wdn_r[:, HI, w, :], wdn[:, k, :]).then_inc(e_dnh, 1)
                    dve.wait_ge(e_dnh, i + 3)
                    dve.tensor_tensor(wdn_r[:, LO, w, :], wdn[:, (j + 2) % RING, :], value(wdn_r[:, HI, w, :]),
                                      ALU.subtract).then_inc(e_dn, 1)

            run_tiles(dve, e_step)

            dve.wait_ge(e_y, TILES)
            for a in (HI, LO):
                ins = dve.memset(value(probT_r[:, a, PT_AT[3]:PT_AT[3] + P]), 0.0)
            ins.then_inc(pad_rdy, 1)

            def a_step(u, j, n):
                if exists(u + 1, UNITS):
                    j1 = (j + 1) % 4
                    h, b = j1 % 2, j1 // 2
                    for which, (hi_done, to, done) in enumerate(((a_qh, qT_r, a_qs), (a_kh, kT_r, a_ks))):
                        dve.wait_ge(hi_done, u + 2)
                        dve.scalar_tensor_tensor(out=to[:, LO, :], in0=banks[6 + which][:, :],
                                                 scalar=bias_qk[:, h, which:which + 1], in1=value(to[:, HI, :]),
                                                 op0=ALU.add, op1=ALU.subtract).then_inc(done, 1)
                if exists(u, UNITS):
                    for m, (bank, at, to, cols) in enumerate(TRANSPOSED):
                        dve.wait_ge(a_pth, 3 * u + 1 + m)
                        dve.tensor_tensor(probT_r[:, LO, to:to + cols], banks[bank][:, at:at + cols],
                                          value(probT_r[:, HI, to:to + cols]), ALU.subtract).then_inc(a_pt, 1)
                    dve.wait_ge(a_exp, 3 * u + 3)
                    dve.reciprocal(rsum[:, j % 2, :], sums[:, j % 2, :]).then_inc(a_rs, 1)
                if isinstance(u, int) and u == UNITS - 1:
                    dve.wait_ge(total, TT)
                if exists(u - 1, UNITS):
                    j0 = (j - 1) % 4
                    dve.wait_ge(a_rs, u)
                    if due(u - 1):
                        dve.wait_ge(a_acc, 2 * (u - 1))
                    for g in range(2):
                        dve.wait_ge(a_out, 2 * (u - 1) + 1 + g)
                        for m in range(2):
                            q = 2 * g + m
                            to = acc[:, (j0 // 2) * QT + q, :]
                            ins = dve.scalar_tensor_tensor(out=to, in0=banks[6 + g][:, m * D:(m + 1) * D],
                                                           scalar=rsum[:, j0 % 2, q:q + 1], in1=to,
                                                           op0=ALU.mult, op1=ALU.add)
                        ins.then_inc(a_acc, 1)
                if exists(u + 1, UNITS):
                    b = (j + 1) % 2
                    for q, bank, at, _ in SCORES:
                        dve.wait_ge(a_s, 3 * (u + 1) + 1 + bank)
                        ins = dve.tensor_reduce(nmax[:, b, q:q + 1], banks[bank][:, at:at + (q + 1) * P],
                                                AX.X, ALU.max, negate=True)
                    ins.then_inc(a_mx, 1)
                    dve.wait_ge(a_mx, u + 2)
                    dve.tensor_scalar(nmaxs[:, b, :], nmax[:, b, :], SCALE, None, ALU.mult).then_inc(a_max, 1)
                    if b == 0:
                        for g in range(2):
                            dve.wait_ge(a_vh, u + 2 + g)
                            to = v_r[:, :, ((j + 1) % 4) // 2, 2 * g:2 * g + 2, :]
                            dve.tensor_tensor(to[:, LO], banks[6 + g][:, :].rearrange("p (t n) -> p t n", t=2),
                                              value(to[:, HI]), ALU.subtract).then_inc(a_vs, 1)
                if exists(u, UNITS):
                    dve.wait_ge(a_pv, u + 1)
                    if due(u):
                        dve.wait_ge(a_out, 2 * u)
                    dve.tensor_copy(oT_r[:, HI, :], banks[5][:, :]).then_inc(a_oth, 1)
                    dve.wait_ge(a_oth, u + 1)
                    dve.tensor_tensor(oT_r[:, LO, :], banks[5][:, :], value(oT_r[:, HI, :]), ALU.subtract).then_inc(a_ot, 1)
                if isinstance(u, int) and u == UNITS - 2:
                    dve.wait_ge(summed, (TOPK - 1) * TT)
                    dve.wait_ge(a_acc, 2 * u)
                    for t in range(TT):
                        dve.tensor_tensor(acc[:, t, :], acc[:, t, :], moe[:, t, :], ALU.add).then_inc(total, 1)

            run_units(dve, a_step)
def exists(index, count):
    return not isinstance(index, int) or 0 <= index < count


def tiles_left(i):
    return min(2, TILES - i) if isinstance(i, int) else 2


def run_shared(step):
    for k in range(-1, SHARED * TT + 1):
        step(k)


def run_tiles(eng, step):
    full = (TILES - 4 - RING) // RING
    for i in range(-4, RING + 1):
        step(i, i % RING, i // RING)
    with eng.Fori(1, full) as n:
        for i in range(1, RING + 1):
            step(n * RING + i, i % RING, n + i // RING)
    for i in range(full * RING + 1, TILES + 3):
        step(i, i % RING, i // RING)


def run_units(eng, step):
    for u in range(-1, 4):
        step(u, u % 4, u // 4)
    with eng.Fori(1, UNITS // 4 - 1) as n:
        for j in range(4):
            step(n * 4 + j, j, n)
    for u in range(UNITS - 4, UNITS + 1):
        step(u, u % 4, u // 4)


def kernel(L0_attn_query, L0_attn_w_q, L0_attn_b_q, L0_attn_w_k, L0_attn_b_k, L0_attn_w_v, L0_attn_b_v,
           L0_attn_w_o, L0_attn_b_o, L0_ffn_gate_w, L0_ffn_shared_gate_w, L0_ffn_w13, L0_ffn_w2,
           L0_ffn_se_gate_up_w, L0_ffn_se_down_w):
    import numpy as np
    import concourse.bacc as bacc
    from concourse.bass_utils import run_bass_kernel_spmd

    f = np.ascontiguousarray

    def by_head(w):
        return np.asarray(w).reshape(HC, P, NH, HD).transpose(2, 1, 0, 3)

    def column(b):
        return np.asarray(b).reshape(NH, HD, 1)

    w_qk = f(np.concatenate([by_head(L0_attn_w_q).reshape(NH, P, HC * HD), by_head(L0_attn_w_k).reshape(NH, P, HC * HD),
                             column(L0_attn_b_q), column(L0_attn_b_k)], axis=2))
    w_v = f(np.asarray(L0_attn_w_v).reshape(HC, P, NH // 2, 2 * HD).transpose(2, 1, 0, 3).reshape(NH // 2, P, HC * 2 * HD))
    w_o = f(np.asarray(L0_attn_w_o).reshape(NH, HD, D))
    gate_up = np.asarray(L0_ffn_se_gate_up_w).reshape(2, SHARED, I, D).transpose(1, 0, 2, 3).reshape(SHARED, 2 * I, D)
    down = np.asarray(L0_ffn_se_down_w).reshape(D, SHARED, I).transpose(1, 0, 2)
    up_all = np.concatenate([np.asarray(L0_ffn_w13), gate_up])
    down_all = np.concatenate([np.asarray(L0_ffn_w2), down])
    w_up = f(up_all.transpose(0, 2, 1).reshape(E + SHARED, HC, P, 2 * I).transpose(0, 2, 1, 3).reshape(E + SHARED, P, HC * 2 * I))
    w_down = f(down_all.transpose(0, 2, 1).reshape(E + SHARED, 2, IH, D).transpose(0, 2, 1, 3).reshape(E + SHARED, IH, 2 * D))
    gates = f(np.concatenate([np.asarray(L0_ffn_gate_w), np.asarray(L0_ffn_shared_gate_w)]).T.reshape(HC, P, E + 1).transpose(1, 0, 2))
    arrays = {
        "x": f(np.asarray(L0_attn_query).reshape(TOK, D)), "w_qk": w_qk, "w_v": w_v, "w_o": w_o,
        "b_v": f(np.asarray(L0_attn_b_v).reshape(NH, HD).T), "b_o": f(np.asarray(L0_attn_b_o).reshape(1, D)),
        "gates": gates, "w_up": w_up, "w_down": w_down,
    }
    nc = bacc.Bacc("TRN2", target_bir_lowering=False, num_devices=1)
    args = [nc.dram_tensor(name, a.shape, mybir.dt.from_np(a.dtype), kind="ExternalInput").ap() for name, a in arrays.items()]
    out = nc.dram_tensor("out", (TOK, D), F32, kind="ExternalOutput").ap()
    layer_kernel(nc, *args, out)
    r = run_bass_kernel_spmd(nc, [arrays], core_ids=[0])
    return r.results[0]["out"].reshape(BATCH, SEQ, D)
```
